# Optimizing a Trainium2 kernel written in Bass

```python
import numpy as np
import jax
import jax.numpy as jnp

def _softmax(x, axis=-1):
    return jax.nn.softmax(x, axis=axis)

def _gelu(x):
    return jax.nn.gelu(x, approximate=True)

def _silu(x):
    return jax.nn.silu(x)

def _sigmoid(x):
    return jax.nn.sigmoid(x)

def _layernorm(x, axis=-1, eps=1e-05):
    m = jnp.mean(x, axis=axis, keepdims=True)
    v = jnp.var(x, axis=axis, keepdims=True)
    return (x - m) / jnp.sqrt(v + eps)

def _scatter_add(tgt, idx, src, axis=0):
    return tgt.at[idx].add(src)

def _segment_sum(src, seg, n):
    return jax.ops.segment_sum(src, seg, n)
kernel_name = 'mk_seq_postln_d1_jaxref_r8_f0b7d1'

def setup_inputs(seed: int=0):
    np.random.seed(seed)
    _w = jnp.asarray

    def _L0_attn_setup():
        import jax, jax.numpy as jnp
        import numpy as np

        def _sin_rpe(Lq, d_model, dtype):
            inv_freq = 1.0 / 10000.0 ** (jnp.arange(0, d_model, 2, dtype=jnp.float32) / d_model)
            pos = jnp.arange(-(Lq - 1), Lq, dtype=jnp.float32)
            ang = pos[:, None] * inv_freq[None, :]
            emb = jnp.zeros((2 * Lq - 1, d_model), dtype=jnp.float32)
            emb = emb.at[:, 0::2].set(jnp.sin(ang)).at[:, 1::2].set(jnp.cos(ang))
            return emb.astype(dtype)

        def _rel_shift(x):
            B, H, Lq, Lr = x.shape
            xp = jnp.concatenate([jnp.zeros((B, H, Lq, 1), x.dtype), x], axis=-1)
            xp = xp.reshape(B, H, Lr + 1, Lq)
            return xp[:, :, 1:].reshape(B, H, Lq, Lr)[..., Lr - Lq:]
        key = jax.random.key(seed)
        ks = jax.random.split(key, 7)
        B, Lq, D, H = (1, 256, 128, 16)
        d_head = D // H
        s = 0.02
        return {'w': jax.random.normal(ks[0], (B, Lq, D), jnp.float32), 'Wq': jax.random.normal(ks[1], (D, D), jnp.float32) * s, 'Wk': jax.random.normal(ks[2], (D, D), jnp.float32) * s, 'Wv': jax.random.normal(ks[3], (D, D), jnp.float32) * s, 'Wr': jax.random.normal(ks[4], (D, D), jnp.float32) * s, 'u_bias': jax.random.normal(ks[5], (H, d_head), jnp.float32) * 0.02, 'v_bias': jax.random.normal(ks[6], (H, d_head), jnp.float32) * 0.02}
    _L0_attn_in = _L0_attn_setup()

    def _L0_ffn_setup():
        import jax, jax.numpy as jnp
        import numpy as np
        key = jax.random.key(seed)
        ks = jax.random.split(key, 7)
        B, N, D, F, E = (4, 256, 128, 512, 8)
        s_in = 1.0 / np.sqrt(D)
        s_ff = 1.0 / np.sqrt(F)
        return {'x': jax.random.normal(ks[0], (B, N, D), dtype=jnp.float32), 'Wg': jax.random.normal(ks[1], (D, E), dtype=jnp.float32) * s_in, 'bg': jnp.zeros((E,), dtype=jnp.float32), 'W1': jax.random.normal(ks[2], (E, D, F), dtype=jnp.float32) * s_in, 'b1': jnp.zeros((E, F), dtype=jnp.float32), 'W2': jax.random.normal(ks[3], (E, F, D), dtype=jnp.float32) * s_ff, 'b2': jnp.zeros((E, D), dtype=jnp.float32)}
    _L0_ffn_in = _L0_ffn_setup()
    _d = {'L0_attn_w': _L0_attn_in['w'], 'L0_attn_Wq': _L0_attn_in['Wq'], 'L0_attn_Wk': _L0_attn_in['Wk'], 'L0_attn_Wv': _L0_attn_in['Wv'], 'L0_attn_Wr': _L0_attn_in['Wr'], 'L0_attn_u_bias': _L0_attn_in['u_bias'], 'L0_attn_v_bias': _L0_attn_in['v_bias'], 'L0_ffn_Wg': _L0_ffn_in['Wg'], 'L0_ffn_bg': _L0_ffn_in['bg'], 'L0_ffn_W1': _L0_ffn_in['W1'], 'L0_ffn_b1': _L0_ffn_in['b1'], 'L0_ffn_W2': _L0_ffn_in['W2'], 'L0_ffn_b2': _L0_ffn_in['b2']}
    _x0 = _d['L0_attn_w']
    _d['L0_attn_w'] = jax.random.normal(jax.random.fold_in(jax.random.key(seed), 1), (16, 256, 128), dtype=_x0.dtype)
    del _x0
    return _d

def reference(L0_attn_w, L0_attn_Wq, L0_attn_Wk, L0_attn_Wv, L0_attn_Wr, L0_attn_u_bias, L0_attn_v_bias, L0_ffn_Wg, L0_ffn_bg, L0_ffn_W1, L0_ffn_b1, L0_ffn_W2, L0_ffn_b2):

    def _L0_attn_ref(w, Wq, Wk, Wv, Wr, u_bias, v_bias):
        import jax, jax.numpy as jnp
        import numpy as np

        def _sin_rpe(Lq, d_model, dtype):
            inv_freq = 1.0 / 10000.0 ** (jnp.arange(0, d_model, 2, dtype=jnp.float32) / d_model)
            pos = jnp.arange(-(Lq - 1), Lq, dtype=jnp.float32)
            ang = pos[:, None] * inv_freq[None, :]
            emb = jnp.zeros((2 * Lq - 1, d_model), dtype=jnp.float32)
            emb = emb.at[:, 0::2].set(jnp.sin(ang)).at[:, 1::2].set(jnp.cos(ang))
            return emb.astype(dtype)

        def _rel_shift(x):
            B, H, Lq, Lr = x.shape
            xp = jnp.concatenate([jnp.zeros((B, H, Lq, 1), x.dtype), x], axis=-1)
            xp = xp.reshape(B, H, Lr + 1, Lq)
            return xp[:, :, 1:].reshape(B, H, Lq, Lr)[..., Lr - Lq:]
        B, Lq, D = w.shape
        H, d_head = u_bias.shape
        scale = 1.0 / np.sqrt(d_head).astype(np.float32)
        r = _sin_rpe(Lq, D, w.dtype)
        q = (w @ Wq.T).reshape(B, Lq, H, d_head).transpose(0, 2, 1, 3)
        k = (w @ Wk.T).reshape(B, Lq, H, d_head).transpose(0, 2, 1, 3)
        v = (w @ Wv.T).reshape(B, Lq, H, d_head).transpose(0, 2, 1, 3)
        rp = (r @ Wr.T).reshape(2 * Lq - 1, H, d_head).transpose(1, 0, 2)
        AC = jnp.einsum('bhid,bhjd->bhij', q + u_bias[None, :, None, :], k)
        BD = jnp.einsum('bhid,hjd->bhij', q + v_bias[None, :, None, :], rp)
        BD = _rel_shift(BD)
        attn = jax.nn.softmax((AC + BD) * scale, axis=-1)
        out = jnp.einsum('bhij,bhjd->bhid', attn, v)
        return out.transpose(0, 2, 1, 3).reshape(B, Lq, D)

    def _L0_ffn_ref(x, Wg, bg, W1, b1, W2, b2):
        import jax, jax.numpy as jnp
        import numpy as np
        TOP_K = 2
        gate_scores = jax.nn.softmax(x @ Wg + bg, axis=-1)
        topk_scores, topk_idx = jax.lax.top_k(gate_scores, TOP_K)
        h = jax.nn.relu(jnp.einsum('bnd,edf->ebnf', x, W1) + b1[:, None, None, :])
        eo = jnp.einsum('ebnf,efd->ebnd', h, W2) + b2[:, None, None, :]
        eo_bne = jnp.transpose(eo, (1, 2, 0, 3))
        gathered = jnp.take_along_axis(eo_bne, topk_idx[..., None], axis=2)
        output = jnp.sum(topk_scores[..., None] * gathered, axis=2)
        return output
    x = L0_attn_w
    x = _layernorm(x + _L0_attn_ref(x, L0_attn_Wq, L0_attn_Wk, L0_attn_Wv, L0_attn_Wr, L0_attn_u_bias, L0_attn_v_bias), axis=-1)
    x = _layernorm(x + _L0_ffn_ref(x, L0_ffn_Wg, L0_ffn_bg, L0_ffn_W1, L0_ffn_b1, L0_ffn_W2, L0_ffn_b2), axis=-1)
    return x

_drawn_inputs = setup_inputs


def setup_inputs(seed=0):
    import zlib

    import numpy as np

    out = dict(_drawn_inputs(seed))
    spreads = {'L0_ffn_bg': (0.0, 0.1), 'L0_ffn_b1': (0.0, 0.275), 'L0_ffn_b2': (0.0, 0.1)}
    factors = {'L0_attn_Wq': 8.0,
     'L0_attn_Wk': 8.0,
     'L0_attn_Wr': 8.0,
     'L0_attn_u_bias': 8.0,
     'L0_attn_v_bias': 24.028}
    for name, (base, spread) in spreads.items():
        noise = np.random.default_rng([zlib.crc32(name.encode()), seed]).standard_normal(out[name].shape)
        drawn = base * np.exp(spread * noise) if base else spread * noise
        out[name] = jnp.asarray(drawn.astype(out[name].dtype))
    for name, factor in factors.items():
        out[name] = (out[name] * factor).astype(out[name].dtype)
    return out
```

```python
from contextlib import ExitStack

import numpy as np

import concourse.bass as bass
from concourse import mybir

F32 = mybir.dt.float32
F32R = mybir.dt.float32r
ALU = mybir.AluOpType
ACT = mybir.ActivationFunctionType
AX = mybir.AxisListType

P = 128
B, L, D = 16, 256, 128
H = 16
DH = D // H
E, F = 8, 512
FC = F // P
TOK = B * L
SCALE = 1.0 / float(np.sqrt(np.float32(DH)))
EPS = 1e-5

NHI = 8
HALF = 2
LO = 16
SHIFT = HALF * LO
NREL = L + SHIFT
REL_PAD = 2 * L
GB = 2
NG = B // GB
STEP_TILES = 4
UNIT_STEPS = LO // STEP_TILES
PAIR = 2
PAIRS = H // PAIR
PAIR_UNITS = PAIR * HALF
PAIR_STEPS = PAIR_UNITS * UNIT_STEPS
STEPS = PAIRS * PAIR_STEPS
VG = 4
VQ = B // VG
VW = 32
PV_LAG = UNIT_STEPS + 1
OUT_LAG = 2 * UNIT_STEPS + 1
TAIL = PV_LAG + 1
TILES = TOK // P
CHUNK = 512
CHUNKS = TOK // CHUNK
CT = CHUNK // P
HN = E * FC


def attention_moe_kernel(nc, w_tok, wT, WqT, WkT, WvT, WrT, u_bias, v_bias, sin_low, sin_up, ident_in, earlier_in,
                         sel_in, Wg, bg, W1, b1T, W2, b2, out):
    with ExitStack() as whole:
        def sem(name):
            return whole.enter_context(nc.semaphore(name))

        def alloc(stack, name, shape, dt=F32):
            return stack.enter_context(nc.sbuf_tensor(name, shape, dt))

        def psum(stack, name, shape):
            return stack.enter_context(nc.psum_tensor(name, shape, F32))

        q_rel_dram = nc.dram_tensor("q_rel_dram", [D, HALF, NHI, 2, 2, B * LO], F32).ap()
        q_key_dram = nc.dram_tensor("q_key_dram", [D, HALF, B, 2 * P], F32).ap()
        key_dram = nc.dram_tensor("key_dram", [D, B, 2 * L], F32).ap()
        rel_dram = nc.dram_tensor("rel_dram", [D, 2, 2, REL_PAD], F32).ap()

        attn = alloc(whole, "attn", [P, TILES, D])
        x_sb = alloc(whole, "x_sb", [P, TILES, D])
        ident = alloc(whole, "ident", [P, P])
        w2_sb = alloc(whole, "w2_sb", [P, E, FC, D])

        att = ExitStack()
        v_all = alloc(att, "v_all", [P, TILES, H, DH + 1])
        q_rel = alloc(att, "q_rel", [P, HALF, 2, NHI, B, LO], F32R)
        q_key = alloc(att, "q_key", [P, HALF, 2, NHI, B, LO], F32R)
        keys = alloc(att, "keys", [P, PAIR, 2, L], F32R)
        rel = alloc(att, "rel", [P, PAIR, 2, NREL], F32R)

        c_loaded = sem("c_loaded")
        wt_loaded = [sem(f"wt_loaded{i}") for i in range(4)]
        biases_scaled = sem("biases_scaled")
        rel_done = sem("rel_done")
        rel_high = sem("rel_high")
        rel_low = sem("rel_low")
        q_done = sem("q_done")
        k_done = sem("k_done")
        v_done = sem("v_done")
        q_full = sem("q_full")
        k_full = sem("k_full")
        v_copied = sem("v_copied")
        high_done = sem("high_done")
        low_done = sem("low_done")
        stored = [sem(f"stored{i}") for i in range(2)]
        rel_stored = sem("rel_stored")
        C_LOADS = 9
        STORES = 6

        with ExitStack() as st:
            wT_sb = attn[:].rearrange("p t d -> p (t d)")
            wq_sb = alloc(st, "wq_sb", [P, D])
            wk_sb = alloc(st, "wk_sb", [P, D])
            wv_sb = alloc(st, "wv_sb", [P, D])
            wr_sb = alloc(st, "wr_sb", [P, D])
            sins = alloc(st, "sins", [P, 2, REL_PAD])
            bias = alloc(st, "bias", [P, 4])
            rel_stage = alloc(st, "rel_stage", [P, 2, 2, REL_PAD], F32R)
            full_v = alloc(st, "full_v", [P, 2, GB, L + SHIFT])
            full_u = alloc(st, "full_u", [P, 2, GB, L])
            full_k = alloc(st, "full_k", [P, 2, GB, L])
            stage_rel = alloc(st, "stage_rel", [P, 2, 2, 2, HALF, NHI, GB, LO], F32R)
            stage_q = alloc(st, "stage_q", [P, 2, HALF, GB, 2, P], F32R)
            stage_k = alloc(st, "stage_k", [P, 2, GB, 2, L], F32R)
            rel_ps = psum(st, "rel_ps", [P, 2, REL_PAD])
            q_ps = psum(st, "q_ps", [P, 2, CHUNK])
            k_ps = psum(st, "k_ps", [P, 2, CHUNK])
            v_ps = psum(st, "v_ps", [P, 2, CT, D])
            block = st.enter_context(nc.Block())

            def rel_view(slot, up, half):
                start = half * LO + up
                return full_v[:, slot, :, start:start + L].rearrange("p b (h x) -> p h b x", x=SHIFT)[:, :, :, 0:LO]

            def key_view(slot, half):
                return full_u[:, slot].rearrange("p b (h a l) -> p b h a l", h=NHI, a=HALF)[:, :, :, half, :]

            @block.sync
            def _(sp):
                sp.dma_start(wq_sb[:], WqT).then_inc(c_loaded, 16)
                sp.dma_start(bias[:, 0:1], u_bias).then_inc(c_loaded, 16)
                sp.dma_start(bias[:, 1:2], v_bias).then_inc(c_loaded, 16)
                sp.dma_start(wk_sb[:], WkT).then_inc(c_loaded, 16)
                sp.dma_start(wv_sb[:], WvT).then_inc(c_loaded, 16)
                sp.dma_start(wr_sb[:], WrT).then_inc(c_loaded, 16)
                sp.dma_start(sins[:, 0, :], sin_low).then_inc(c_loaded, 16)
                sp.dma_start(sins[:, 1, :], sin_up).then_inc(c_loaded, 16)
                sp.dma_start(ident[:], ident_in).then_inc(c_loaded, 16)
                for c in range(4):
                    part = slice(c * 1024, (c + 1) * 1024)
                    sp.dma_start(wT_sb[:, part], wT[:, part]).then_inc(wt_loaded[c], 16)
                sp.wait_ge(rel_low, 1)
                sp.dma_start(rel_dram.rearrange("p a b x -> p (a b x)"),
                             rel_stage[:].bitcast(F32).rearrange("p a b x -> p (a b x)")).then_inc(rel_stored, 16)
                for c in range(NG):
                    slot = c % 2
                    sp.wait_ge(high_done, c + 1)
                    sp.wait_ge(low_done, c + 1)
                    for up in range(2):
                        for part in range(2):
                            sp.dma_start(
                                q_rel_dram[:, :, :, up, part, c * GB * LO:(c + 1) * GB * LO].rearrange(
                                    "p a b x -> p (a b) x"),
                                stage_rel[:, slot, up, part].bitcast(F32).rearrange(
                                    "p a b q x -> p (a b) (q x)")).then_inc(stored[slot], 16)
                    sp.dma_start(
                        q_key_dram[:, :, c * GB:(c + 1) * GB, :].rearrange("p a b x -> p a (b x)"),
                        stage_q[:, slot].bitcast(F32).rearrange("p a b l x -> p a (b l x)")).then_inc(stored[slot], 16)
                    sp.dma_start(
                        key_dram[:, c * GB:(c + 1) * GB, :].rearrange("p b x -> p (b x)"),
                        stage_k[:, slot].bitcast(F32).rearrange("p b l x -> p (b l x)")).then_inc(stored[slot], 16)
                for slot in range(2):
                    sp.wait_ge(stored[slot], 16 * STORES * (NG // 2))
                sp.wait_ge(rel_stored, 16)

            @block.tensor
            def _(pe):
                pe.wait_ge(c_loaded, 16 * C_LOADS)
                for c in range(NG):
                    slot = c % 2
                    if c % 2 == 0:
                        pe.wait_ge(wt_loaded[c // 2], 16)
                    cols = wT_sb[:, c * CHUNK:(c + 1) * CHUNK]
                    if c >= 2:
                        pe.wait_ge(q_full, c - 1)
                    nc.tensor.matmul(q_ps[:, slot, :], wq_sb[:], cols, start=True, stop=True).then_inc(q_done, 1)
                    if c >= 2:
                        pe.wait_ge(k_full, c - 1)
                    nc.tensor.matmul(k_ps[:, slot, :], wk_sb[:], cols, start=True, stop=True).then_inc(k_done, 1)
                    if c >= 2:
                        pe.wait_ge(v_copied, c - 1)
                    for t in range(CT):
                        last = nc.tensor.matmul(v_ps[:, slot, t, :], cols[:, t * P:(t + 1) * P], wv_sb[:],
                                                start=True, stop=True)
                    last.then_inc(v_done, 1)
                    if c == 0:
                        for up in range(2):
                            last = nc.tensor.matmul(rel_ps[:, up, :], wr_sb[:], sins[:, up, :], start=True, stop=True)
                        last.then_inc(rel_done, 1)

            @block.scalar
            def _(act):
                act.wait_ge(biases_scaled, 1)
                for c in range(NG):
                    slot = c % 2
                    if c >= 2:
                        act.wait_ge(low_done, c - 1)
                        act.wait_ge(stored[slot], 16 * STORES * (c // 2))
                    act.wait_ge(q_done, c + 1)
                    src = q_ps[:, slot, :].rearrange("p (b i) -> p b i", b=GB)
                    nc.scalar.activation(full_u[:, slot], src, ACT.Identity, bias=bias[:, 2:3], scale=SCALE)
                    nc.scalar.activation(full_v[:, slot, :, 0:L], src, ACT.Identity,
                                         bias=bias[:, 3:4], scale=SCALE).then_inc(q_full, 1)
                    act.wait_ge(k_done, c + 1)
                    nc.scalar.copy(full_k[:, slot], k_ps[:, slot, :].rearrange("p (b i) -> p b i", b=GB)).then_inc(
                        k_full, 1)
                    act.wait_ge(q_full, c + 1)
                    act.wait_ge(k_full, c + 1)
                    for up in range(2):
                        for half in range(HALF):
                            nc.scalar.copy(stage_rel[:, slot, up, 0, half], rel_view(slot, up, half))
                    for half in range(HALF):
                        nc.scalar.copy(stage_q[:, slot, half, :, 0, :].rearrange("p b (h l) -> p b h l", h=NHI),
                                       key_view(slot, half))
                    nc.scalar.copy(stage_k[:, slot, :, 0, :], full_k[:, slot]).then_inc(high_done, 1)
                    if c == 0:
                        act.wait_ge(rel_done, 1)
                        nc.scalar.copy(rel_stage[:, :, 0, :], rel_ps[:]).then_inc(rel_high, 1)

            @block.vector
            def _(dve):
                nc.vector.memset(full_v[:, :, :, L:L + SHIFT], 0.0)
                nc.vector.memset(v_all[:, :, :, DH:DH + 1], 1.0)
                dve.wait_ge(c_loaded, 16 * C_LOADS)
                nc.vector.tensor_scalar(bias[:, 2:4], bias[:, 0:2], SCALE, None, ALU.mult).then_inc(biases_scaled, 1)
                for c in range(NG):
                    slot = c % 2
                    dve.wait_ge(v_done, c + 1)
                    nc.vector.tensor_copy(v_all[:, CT * c:CT * (c + 1), :, 0:DH],
                                          v_ps[:, slot].rearrange("p t (h d) -> p t h d", h=H)).then_inc(v_copied, 1)
                    dve.wait_ge(high_done, c + 1)
                    for up in range(2):
                        for half in range(HALF):
                            nc.vector.tensor_tensor(stage_rel[:, slot, up, 1, half], rel_view(slot, up, half),
                                                    stage_rel[:, slot, up, 0, half].bitcast(F32), ALU.subtract)
                    for half in range(HALF):
                        low = stage_q[:, slot, half, :, 1, :].rearrange("p b (h l) -> p b h l", h=NHI)
                        high = stage_q[:, slot, half, :, 0, :].bitcast(F32).rearrange("p b (h l) -> p b h l", h=NHI)
                        nc.vector.tensor_tensor(low, key_view(slot, half), high, ALU.subtract)
                    nc.vector.tensor_tensor(stage_k[:, slot, :, 1, :], full_k[:, slot],
                                            stage_k[:, slot, :, 0, :].bitcast(F32),
                                            ALU.subtract).then_inc(low_done, 1)
                    if c == 0:
                        dve.wait_ge(rel_high, 1)
                        nc.vector.tensor_tensor(rel_stage[:, :, 1, :], rel_ps[:],
                                                rel_stage[:, :, 0, :].bitcast(F32),
                                                ALU.subtract).then_inc(rel_low, 1)

            @block.gpsimd
            def _(pool):
                nc.gpsimd.memset(q_rel[:].bitcast(F32), 0.0)
                nc.gpsimd.memset(q_key[:].bitcast(F32), 0.0)

        q_loaded = [sem(f"q_loaded{i}") for i in range(HALF)]
        head_loaded = [sem(f"head_loaded{i}") for i in range(PAIR)]
        x_loaded = sem("x_loaded")
        scores_done = sem("scores_done")
        max_done = sem("max_done")
        exp_done = sem("exp_done")
        turned = sem("turned")
        turned_copied = sem("turned_copied")
        pv_done = sem("pv_done")
        o_copied = sem("o_copied")
        o_turned = sem("o_turned")
        recip_done = sem("recip_done")
        o_scaled = sem("o_scaled")
        v_padded = sem("v_padded")
        v_ready = sem("v_ready")
        Q_LOADED = 16 * (NHI + B)
        HEAD_LOADED = 16 * (NHI + 1)

        with ExitStack() as st:
            probsT = alloc(st, "probsT", [P, 2, 2, NHI, B, LO])
            probs = alloc(st, "probs", [P, 2, STEP_TILES, L])
            v_head = alloc(st, "v_head", [P, PAIR, TILES, VW])
            o_sb = alloc(st, "o_sb", [P, VQ, P])
            neg_max = alloc(st, "neg_max", [P, 2, STEP_TILES])
            recip = alloc(st, "recip", [P, B])
            s_ps = psum(st, "s_ps", [P, 2, STEP_TILES, L])
            t_ps = psum(st, "t_ps", [P, 2, 2, 2, P])
            o_ps = psum(st, "o_ps", [P, VQ, P])
            ot_ps = psum(st, "ot_ps", [P, VQ, VG, VW])
            block = st.enter_context(nc.Block())

            def each_step(eng, step):
                for k in range(PAIR_STEPS):
                    step(0, k, k)
                with eng.Fori(1, PAIRS) as pair:
                    for k in range(PAIR_STEPS):
                        step(pair, k, PAIR_STEPS + k)
                for k in range(TAIL):
                    step(PAIRS, k, STEPS + k)

            @block.sync
            def _(sp):
                def load_pair(pair, first):
                    for k in range(PAIR_UNITS):
                        hd = k // HALF
                        half = k % HALF
                        rows = bass.ds(pair * (PAIR * DH) + hd * DH, DH)
                        if not (first and k < 2):
                            sp.wait_ge(scores_done, pair * PAIR_STEPS + (k - 1) * UNIT_STEPS)
                        if half == 0:
                            sp.dma_start(
                                keys[:, hd].bitcast(F32).rearrange("p a x -> p (a x)"),
                                key_dram[rows].rearrange("d b x -> b d x")).then_inc(head_loaded[hd], 16)
                            for hi in range(NHI):
                                r = hi * 2 * DH
                                first_col = L - SHIFT - SHIFT * hi
                                sp.dma_start(
                                    rel[r:r + 2 * DH, hd].bitcast(F32),
                                    rel_dram[rows, :, :, first_col:first_col + NREL].rearrange(
                                        "d u a x -> (d u) a x")).then_inc(head_loaded[hd], 16)
                        for hi in range(NHI):
                            r = hi * 2 * DH
                            sp.dma_start(
                                q_rel[r:r + 2 * DH, half, :, hi].bitcast(F32).rearrange("p a b x -> p a (b x)"),
                                q_rel_dram[rows, half, hi].rearrange("d u a x -> d u (a x)")).then_inc(
                                    q_loaded[half], 16)
                        for b in range(B):
                            sp.dma_start(
                                q_key[b * DH:(b + 1) * DH, half, :, :, b].bitcast(F32).rearrange(
                                    "p a h x -> p (a h) x"),
                                q_key_dram[rows, half, b].rearrange("d (a x) -> d a x", x=LO)).then_inc(
                                    q_loaded[half], 16)

                load_pair(0, True)
                sp.dma_start(x_sb[:], w_tok.rearrange("t p d -> p t d")).then_inc(x_loaded, 16)
                sp.dma_start(w2_sb[:], W2.rearrange("e (c p) d -> p e c d", p=P)).then_inc(x_loaded, 16)
                with sp.Fori(1, PAIRS) as pair:
                    load_pair(pair, False)

            @block.gpsimd
            def _(pool):
                nc.gpsimd.memset(v_head[:], 0.0).then_inc(v_padded, 1)
                pool.wait_ge(v_padded, 1)

                def values(pair, first):
                    for hd in range(PAIR):
                        if not first:
                            pool.wait_ge(pv_done, pair * PAIR_STEPS + (hd - 1) * HALF * UNIT_STEPS)
                        nc.gpsimd.tensor_copy(v_head[:, hd, :, 0:DH + 1],
                                              v_all[:, :, bass.ds(pair * PAIR + hd, 1), :].rearrange(
                                                  "p t h d -> p t (h d)")).then_inc(v_ready, 1)

                values(0, True)
                with pool.Fori(1, PAIRS) as pair:
                    values(pair, False)

            @block.tensor
            def _(pe):
                def scores(pair, k, at):
                    unit = k // UNIT_STEPS
                    half = unit % HALF
                    hd = unit // HALF
                    if k % UNIT_STEPS == 0:
                        pe.wait_ge(q_loaded[half], pair * (PAIR * Q_LOADED) + (unit // HALF + 1) * Q_LOADED)
                        if half == 0:
                            pe.wait_ge(head_loaded[hd], pair * HEAD_LOADED + HEAD_LOADED)
                    if at >= 2:
                        pe.wait_ge(exp_done, pair * PAIR_STEPS + (k - 1))
                    for t in range(STEP_TILES):
                        lo = (k % UNIT_STEPS) * STEP_TILES + t
                        start = SHIFT - 1 - (half * LO + lo)
                        q_r = [q_rel[:, half, x, :, :, lo].rearrange("p h b -> p (h b)") for x in range(2)]
                        r = [rel[:, hd, x, start:start + L] for x in range(2)]
                        q_k = [q_key[:, half, x, :, :, lo].rearrange("p h b -> p (h b)") for x in range(2)]
                        ks = [keys[:, hd, x, :] for x in range(2)]
                        o = s_ps[:, k % 2, t, :]
                        nc.tensor.matmul(o, q_r[0], r[0], start=True, stop=False)
                        nc.tensor.matmul(o, q_r[0], r[1], start=False, stop=False)
                        nc.tensor.matmul(o, q_r[1], r[0], start=False, stop=False)
                        nc.tensor.matmul(o, q_k[0], ks[0], start=False, stop=False)
                        nc.tensor.matmul(o, q_k[0], ks[1], start=False, stop=False)
                        last = nc.tensor.matmul(o, q_k[1], ks[0], start=False, stop=True)
                    last.then_inc(scores_done, 1)

                def turn_out(pair, k, at):
                    n = (k - OUT_LAG) // UNIT_STEPS
                    pe.wait_ge(o_copied, pair * PAIR_UNITS + (n + 1))
                    if at > OUT_LAG:
                        pe.wait_ge(o_scaled, pair * PAIR_UNITS + n)
                    for q in range(VQ):
                        last = nc.tensor.transpose(ot_ps[:, q].rearrange("p g e -> p (g e)"), o_sb[:, q], ident[:])
                    last.then_inc(o_turned, 1)

                def values(pair, k, at):
                    v = k - PV_LAG
                    q = v % UNIT_STEPS
                    unit = v // UNIT_STEPS
                    hd = (unit // HALF) % PAIR
                    if q == 0:
                        pe.wait_ge(turned_copied, pair * (2 * PAIR_STEPS) + 2 * (v + UNIT_STEPS))
                        pe.wait_ge(v_ready, pair * PAIR + (unit // HALF + 1))
                        if at >= PV_LAG + UNIT_STEPS:
                            pe.wait_ge(o_copied, pair * PAIR_UNITS + unit)
                    for g in range(VG):
                        b = q * VG + g
                        for jh in range(2):
                            last = nc.tensor.matmul(
                                o_ps[g * VW:(g + 1) * VW, q, :], v_head[:, hd, 2 * b + jh, :],
                                probsT[:, unit % 2, jh, :, b, :],
                                start=jh == 0, stop=jh == 1)
                    last.then_inc(pv_done, 1)

                def turn_probs(pair, k, at):
                    pe.wait_ge(exp_done, pair * PAIR_STEPS + k)
                    for c in range(2):
                        if at >= 2:
                            pe.wait_ge(turned_copied, pair * (2 * PAIR_STEPS) + (2 * (k - 1) + c - 1))
                        for t in range(2):
                            for jh in range(2):
                                last = nc.tensor.transpose(t_ps[:, c, t, jh, :],
                                                           probs[:, (k - 1) % 2, 2 * c + t, jh * P:(jh + 1) * P],
                                                           ident[:])
                        last.then_inc(turned, 1)

                def step(pair, k, at):
                    if at < STEPS:
                        scores(pair, k, at)
                    if at >= OUT_LAG and (k - OUT_LAG) % UNIT_STEPS == 0:
                        turn_out(pair, k, at)
                    if PV_LAG <= at < STEPS + PV_LAG:
                        values(pair, k, at)
                    if 1 <= at <= STEPS:
                        turn_probs(pair, k, at)

                each_step(pe, step)

            @block.vector
            def _(dve):
                def step(pair, k, at):
                    if at < STEPS:
                        dve.wait_ge(scores_done, pair * PAIR_STEPS + (k + 1))
                        nc.vector.tensor_reduce(neg_max[:, k % 2, :], s_ps[:, k % 2], axis=AX.X, op=ALU.max,
                                                negate=True).then_inc(max_done, 1)
                    if 1 <= at <= STEPS:
                        v = k - 1
                        unit = v // UNIT_STEPS
                        for c in range(2):
                            if v % UNIT_STEPS == 0 and c == 0 and at > 2 * UNIT_STEPS:
                                dve.wait_ge(pv_done, pair * PAIR_STEPS + (unit - 1) * UNIT_STEPS)
                            dve.wait_ge(turned, pair * (2 * PAIR_STEPS) + (2 * v + c + 1))
                            lo = (v % UNIT_STEPS) * STEP_TILES + 2 * c
                            nc.vector.tensor_copy(
                                probsT[:, unit % 2, :, :, :, lo:lo + 2].rearrange("p j h b t -> p t j (h b)"),
                                t_ps[:, c]).then_inc(turned_copied, 1)
                    if at >= OUT_LAG and (k - OUT_LAG) % UNIT_STEPS == 0:
                        n = (k - OUT_LAG) // UNIT_STEPS
                        dve.wait_ge(o_turned, pair * PAIR_UNITS + (n + 1))
                        sums = ot_ps[:].rearrange("p q g e -> p (q g) e")
                        nc.vector.reciprocal(recip[:], sums[:, :, DH]).then_inc(recip_done, 1)
                        dve.wait_ge(recip_done, pair * PAIR_UNITS + (n + 1))
                        head_cols = bass.ds(pair * (PAIR * DH) + (n // HALF) * DH, DH)
                        dst = attn[:].rearrange("p (b a) d -> p b a d", a=HALF)[:, :, n % HALF, head_cols]
                        nc.vector.tensor_tensor(dst, sums[:, :, 0:DH], recip[:].unsqueeze(2).to_broadcast([P, B, DH]),
                                                ALU.mult).then_inc(o_scaled, 1)

                each_step(dve, step)

            @block.scalar
            def _(act):
                def step(pair, k, at):
                    if at < STEPS:
                        act.wait_ge(max_done, pair * PAIR_STEPS + (k + 1))
                        if at >= 2:
                            act.wait_ge(turned, pair * (2 * PAIR_STEPS) + 2 * (k - 1))
                        for t in range(STEP_TILES):
                            last = nc.scalar.activation(probs[:, k % 2, t, :], s_ps[:, k % 2, t, :], ACT.Exp,
                                                        bias=neg_max[:, k % 2, t:t + 1], scale=1.0)
                        last.then_inc(exp_done, 1)
                    if at >= 2 * UNIT_STEPS and k % UNIT_STEPS == 0:
                        n = k // UNIT_STEPS - 2
                        act.wait_ge(pv_done, pair * PAIR_STEPS + (n + 1) * UNIT_STEPS)
                        if at > 2 * UNIT_STEPS:
                            act.wait_ge(o_turned, pair * PAIR_UNITS + n)
                        nc.scalar.copy(o_sb[:], o_ps[:]).then_inc(o_copied, 1)

                each_step(act, step)

        att.close()

        more_loaded = sem("more_loaded")
        chain = sem("chain")
        var_ready = sem("var_ready")
        root_done = sem("root_done")
        normed = sem("normed")
        x_turned = sem("x_turned")
        x_high = sem("x_high")
        x_low = sem("x_low")
        x_copied = sem("x_copied")
        w1_high = sem("w1_high")
        logits_done = sem("logits_done")
        shifted = sem("shifted")
        exp_gates = sem("exp_gates")
        gates_split = sem("gates_split")
        g_turned = sem("g_turned")
        g_copied = sem("g_copied")
        MORE = 7

        ffn = ExitStack()
        w1h = alloc(ffn, "w1h", [P, E, F], F32R)
        w1l = alloc(ffn, "w1l", [P, E, F], F32R)
        b1_sb = alloc(ffn, "b1_sb", [P, HN])
        xh = alloc(ffn, "xh", [P, TOK], F32R)
        xl = alloc(ffn, "xl", [P, TOK], F32R)
        gT = alloc(ffn, "gT", [2 * E, TOK], F32R)
        sel = alloc(ffn, "sel", [2 * E, E, P], F32R)
        b2_sb = alloc(ffn, "b2_sb", [2 * E, D])

        with ExitStack() as st:
            w1_sb = alloc(st, "w1_sb", [P, E, F])
            sel_raw = alloc(st, "sel_raw", [2 * E, E, P])
            wg_sb = alloc(st, "wg_sb", [P, E])
            bg_sb = alloc(st, "bg_sb", [P, E])
            earlier = alloc(st, "earlier", [P, E * E])
            stats = alloc(st, "stats", [P, TILES, 6])
            mv = alloc(st, "mv", [P, TILES, 2])
            var = alloc(st, "var", [P, TILES])
            root = alloc(st, "root", [P, TILES])
            rstd = alloc(st, "rstd", [P, TILES])
            xfull = alloc(st, "xfull", [P, 2, CT, P])
            logit = alloc(st, "logit", [P, TILES, E])
            gate = alloc(st, "gate", [P, TILES, E])
            red = alloc(st, "red", [P, 3, TILES])
            above = alloc(st, "above", [P, TILES, E, E])
            equal = alloc(st, "equal", [P, TILES, E, E])
            rank = alloc(st, "rank", [P, TILES, E])
            gate_split = alloc(st, "gate_split", [P, TILES, E, 2])
            xt_ps = psum(st, "xt_ps", [P, 4, CT, P])
            l_ps = psum(st, "l_ps", [P, 512])
            g_ps = psum(st, "g_ps", [2 * E, 2, CHUNK])
            block = st.enter_context(nc.Block())

            @block.sync
            def _(sp):
                sp.wait_ge(x_loaded, 32)
                sp.dma_start(wg_sb[:], Wg).then_inc(more_loaded, 16)
                sp.dma_start(bg_sb[:], bg.partition_broadcast(P)).then_inc(more_loaded, 16)
                sp.dma_start(earlier[:], earlier_in).then_inc(more_loaded, 16)
                sp.dma_start(sel_raw[:], sel_in).then_inc(more_loaded, 16)
                sp.dma_start(b1_sb[:], b1T).then_inc(more_loaded, 16)
                sp.dma_start(b2_sb[:], b2).then_inc(more_loaded, 16)
                sp.dma_start(w1_sb[:], W1.rearrange("e d f -> d e f")).then_inc(more_loaded, 16)

            @block.gpsimd
            def _(pool):
                pool.wait_ge(w1_high, 1)
                nc.gpsimd.tensor_tensor(w1l[:], w1_sb[:], w1h[:].bitcast(F32), ALU.subtract)

            @block.vector
            def _(dve):
                links = [0]

                def link(ins):
                    links[0] += 1
                    ins.then_inc(chain, 1)
                    dve.wait_ge(chain, links[0])

                dve.wait_ge(x_loaded, 32)
                link(nc.vector.tensor_tensor(attn[:], attn[:], x_sb[:], ALU.add))
                for t in range(TILES):
                    last = nc.vector.bn_stats(stats[:, t, :], attn[:, t, :])
                link(last)
                for t in range(TILES):
                    last = nc.vector.bn_aggr(mv[:, t, :], stats[:, t, :])
                link(last)
                nc.vector.tensor_scalar(var[:], mv[:, :, 1], EPS, None, ALU.add).then_inc(var_ready, 1)
                dve.wait_ge(root_done, 1)
                link(nc.vector.reciprocal(rstd[:], root[:]))
                for t in range(TILES):
                    nc.vector.tensor_scalar(x_sb[:, t, :], attn[:, t, :], mv[:, t, 0:1], rstd[:, t:t + 1],
                                            ALU.subtract, ALU.mult).then_inc(normed, 1)
                dve.wait_ge(more_loaded, 16 * MORE)
                nc.vector.tensor_copy(w1h[:], w1_sb[:]).then_inc(w1_high, 1)
                nc.vector.tensor_copy(sel[:], sel_raw[:])
                for c in range(CHUNKS):
                    dve.wait_ge(x_high, c + 1)
                    dve.wait_ge(x_copied, c + 1)
                    cols = slice(c * CHUNK, (c + 1) * CHUNK)
                    nc.vector.tensor_tensor(xl[:, cols], xfull[:, c % 2].rearrange("p a b -> p (a b)"),
                                            xh[:, cols].bitcast(F32), ALU.subtract).then_inc(x_low, 1)
                dve.wait_ge(logits_done, CHUNKS)
                link(nc.vector.tensor_tensor(logit[:], l_ps[:, 0:TILES * E].rearrange("p (t e) -> p t e", e=E),
                                             bg_sb[:].unsqueeze(1).to_broadcast([P, TILES, E]), ALU.add))
                link(nc.vector.tensor_reduce(red[:, 0], logit[:], axis=AX.X, op=ALU.max))
                nc.vector.tensor_tensor(logit[:], logit[:], red[:, 0].unsqueeze(2).to_broadcast([P, TILES, E]),
                                        ALU.subtract).then_inc(shifted, 1)
                dve.wait_ge(exp_gates, 1)
                link(nc.vector.tensor_reduce(red[:, 1], gate[:], axis=AX.X, op=ALU.add))
                link(nc.vector.reciprocal(red[:, 2], red[:, 1]))
                link(nc.vector.tensor_tensor(gate[:], gate[:], red[:, 2].unsqueeze(2).to_broadcast([P, TILES, E]),
                                             ALU.mult))
                for e in range(E):
                    mine = gate[:, :, e:e + 1].to_broadcast([P, TILES, E])
                    nc.vector.tensor_tensor(above[:, :, e, :], gate[:], mine, ALU.is_gt)
                    last = nc.vector.tensor_tensor(equal[:, :, e, :], gate[:], mine, ALU.is_equal)
                link(last)
                equal_flat = equal[:].rearrange("p t a b -> p t (a b)")
                link(nc.vector.tensor_tensor(equal_flat, equal_flat,
                                             earlier[:].unsqueeze(1).to_broadcast([P, TILES, E * E]), ALU.mult))
                link(nc.vector.tensor_tensor(equal_flat, equal_flat, above[:].rearrange("p t a b -> p t (a b)"),
                                             ALU.add))
                link(nc.vector.tensor_reduce(rank[:], equal[:], axis=AX.X, op=ALU.add))
                link(nc.vector.scalar_tensor_tensor(gate[:], rank[:], 2.0, gate[:], ALU.is_lt, ALU.mult))
                link(nc.vector.tensor_copy(gate_split[:, :, :, 0].bitcast(F32R), gate[:]))
                nc.vector.tensor_tensor(gate_split[:, :, :, 1], gate[:], gate_split[:, :, :, 0],
                                        ALU.subtract).then_inc(gates_split, 1)

            @block.scalar
            def _(act):
                act.wait_ge(var_ready, 1)
                nc.scalar.activation(root[:], var[:], ACT.Sqrt).then_inc(root_done, 1)
                for c in range(CHUNKS):
                    act.wait_ge(x_turned, c + 1)
                    if c >= 2:
                        act.wait_ge(logits_done, c - 1)
                        act.wait_ge(x_low, c - 1)
                    nc.scalar.copy(xh[:, c * CHUNK:(c + 1) * CHUNK],
                                   xt_ps[:, c % 4].rearrange("p a b -> p (a b)")).then_inc(x_high, 1)
                    nc.scalar.copy(xfull[:, c % 2], xt_ps[:, c % 4]).then_inc(x_copied, 1)
                act.wait_ge(shifted, 1)
                nc.scalar.activation(gate[:], logit[:], ACT.Exp).then_inc(exp_gates, 1)
                for c in range(CHUNKS):
                    act.wait_ge(g_turned, c + 1)
                    nc.scalar.copy(gT[:, c * CHUNK:(c + 1) * CHUNK], g_ps[:, c % 2, :]).then_inc(g_copied, 1)

            @block.tensor
            def _(pe):
                def logits(c):
                    pe.wait_ge(x_copied, c + 1)
                    for t in range(CT):
                        n = c * CT + t
                        last = nc.tensor.matmul(l_ps[:, n * E:(n + 1) * E], xfull[:, c % 2, t, :], wg_sb[:],
                                                start=True, stop=True)
                    last.then_inc(logits_done, 1)

                pe.wait_ge(more_loaded, 16 * MORE)
                for c in range(CHUNKS):
                    pe.wait_ge(normed, CT * (c + 1))
                    if c >= 4:
                        pe.wait_ge(x_high, c - 3)
                        pe.wait_ge(x_copied, c - 3)
                    for t in range(CT):
                        last = nc.tensor.transpose(xt_ps[:, c % 4, t, :], x_sb[:, CT * c + t, :], ident[:])
                    last.then_inc(x_turned, 1)
                    if c:
                        logits(c - 1)
                logits(CHUNKS - 1)
                pe.wait_ge(gates_split, 1)
                for c in range(CHUNKS):
                    if c >= 2:
                        pe.wait_ge(g_copied, c - 1)
                    for t in range(CT):
                        last = nc.tensor.transpose(g_ps[:, c % 2, t * P:(t + 1) * P],
                                                   gate_split[:, CT * c + t].rearrange("p e l -> p (e l)"), ident[:])
                    last.then_inc(g_turned, 1)

        h_done = sem("h_done")
        h_relu = sem("h_relu")
        h_used = sem("h_used")
        gate_spread = sem("gate_spread")
        gate_read = sem("gate_read")
        bias_spread = sem("bias_spread")
        acc_begun = sem("acc_begun")
        y_done = sem("y_done")
        y_gated = sem("y_gated")
        acc_added = sem("acc_added")
        y_turned = sem("y_turned")
        y_read = sem("y_read")
        chain4 = sem("chain4")
        var4 = sem("var4")
        root4 = sem("root4")
        out_ready = sem("out_ready")
        out_stored = [sem(f"out_stored{i}") for i in range(2)]
        LAGH = 2
        OUT_AT = 12
        LINKS = 3

        with ExitStack() as st:
            h_sb = alloc(st, "h_sb", [P, 4, CHUNK])
            gate_sb = alloc(st, "gate_sb", [P, 2, CHUNK])
            gated = alloc(st, "gated", [P, 2, CHUNK])
            acc = alloc(st, "acc", [P, 2, CHUNK])
            z_sb = alloc(st, "z_sb", [P, CT, D])
            out_sb = alloc(st, "out_sb", [P, 2, CT, D])
            stats4 = alloc(st, "stats4", [P, CT, 6])
            mv4 = alloc(st, "mv4", [P, CT, 2])
            var_sb = alloc(st, "var_sb", [P, CT])
            root_sb = alloc(st, "root_sb", [P, CT])
            rstd_sb = alloc(st, "rstd_sb", [P, CT])
            pause = alloc(st, "pause", [P, 1])
            h_ps = psum(st, "h_ps", [P, 4, CHUNK])
            y_ps = psum(st, "y_ps", [P, 2, CHUNK])
            spread_ps = psum(st, "spread_ps", [P, CHUNK])
            yt_ps = psum(st, "yt_ps", [P, CT, P])
            block = st.enter_context(nc.Block())

            def each_chunk(eng, chunk):
                for s in range(2):
                    chunk(0, s, s > 0, True)
                with eng.Fori(1, CHUNKS // 2) as pair:
                    for s in range(2):
                        chunk(pair, s, True, True)
                chunk(CHUNKS // 2, 0, True, False)

            @block.tensor
            def _(pe):
                def turn(c, s):
                    pe.wait_ge(acc_added, c * E)
                    if not isinstance(c, int) or c > 1:
                        pe.wait_ge(y_read, c - 1)
                    for t in range(CT):
                        last = nc.tensor.transpose(yt_ps[:, t, :], acc[:, 1 - s, t * P:(t + 1) * P], ident[:])
                    last.then_inc(y_turned, 1)

                def chunk(pair, s, before, now):
                    c = pair * 2 + s
                    if not now:
                        turn(c, s)
                        return
                    cols = bass.ds(c * CHUNK, CHUNK)
                    for n in range(HN + LAGH):
                        if n < HN:
                            e = n // FC
                            part = slice((n % FC) * P, (n % FC + 1) * P)
                            if before or n >= 4:
                                pe.wait_ge(h_relu, c * HN + (n - 3))
                            if n == 0 and before:
                                pe.wait_ge(gate_read, c * E)
                            if n == 2:
                                pe.wait_ge(acc_begun, c + 1)
                            elif n % FC == 2:
                                pe.wait_ge(gate_read, c * E + e)
                            o = h_ps[:, n % 4, :]
                            nc.tensor.matmul(o, w1h[:, e, part], xh[:, cols], start=True, stop=False)
                            nc.tensor.matmul(o, w1h[:, e, part], xl[:, cols], start=False, stop=False)
                            nc.tensor.matmul(o, w1l[:, e, part], xh[:, cols], start=False,
                                             stop=True).then_inc(h_done, 1)
                            if n == 0:
                                nc.tensor.matmul(spread_ps[:], b2_sb[:], gT[:, cols].bitcast(F32), start=True,
                                                 stop=True).then_inc(bias_spread, 1)
                            if n % FC == 2:
                                nc.tensor.matmul(spread_ps[:], sel[:, e, :], gT[:, cols], start=True,
                                                 stop=True).then_inc(gate_spread, 1)
                        if n >= LAGH:
                            m = n - LAGH
                            e = m // FC
                            pe.wait_ge(h_relu, c * HN + (m + 1))
                            if m % FC == 0 and (before or e >= 2):
                                pe.wait_ge(y_gated, c * E + (e - 1))
                            last = nc.tensor.matmul(y_ps[:, e % 2, :], w2_sb[:, e, m % FC, :], h_sb[:, m % 4, :],
                                                    start=m % FC == 0, stop=m % FC == FC - 1)
                            last.then_inc(h_used, 1)
                        if n == OUT_AT and before:
                            turn(c, s)

                each_chunk(pe, chunk)

            @block.scalar
            def _(act):
                def root(c):
                    act.wait_ge(var4, c)
                    nc.scalar.activation(root_sb[:], var_sb[:], ACT.Sqrt).then_inc(root4, 1)

                def chunk(pair, s, before, now):
                    c = pair * 2 + s
                    if not now:
                        root(c)
                        return
                    act.wait_ge(bias_spread, c + 1)
                    if not isinstance(c, int):
                        act.wait_ge(y_turned, c - 1)
                    nc.scalar.copy(acc[:, s, :], spread_ps[:]).then_inc(acc_begun, 1)
                    for n in range(HN):
                        e = n // FC
                        act.wait_ge(h_done, c * HN + (n + 1))
                        if before or n >= 4:
                            act.wait_ge(h_used, c * HN + (n - 3))
                        nc.scalar.activation(h_sb[:, n % 4, :], h_ps[:, n % 4, :], ACT.Relu,
                                             bias=b1_sb[:, n:n + 1], scale=1.0).then_inc(h_relu, 1)
                        if n % FC == 3:
                            act.wait_ge(gate_spread, c * E + (e + 1))
                            if before or e >= 2:
                                act.wait_ge(y_gated, c * E + (e - 1))
                            nc.scalar.copy(gate_sb[:, e % 2, :], spread_ps[:]).then_inc(gate_read, 1)
                        if n == OUT_AT + 8 and before:
                            root(c)

                each_chunk(act, chunk)

            @block.vector
            def _(dve):
                def finish(c, s):
                    link = (c - 1) * LINKS
                    dve.wait_ge(y_turned, c)
                    nc.vector.tensor_tensor(z_sb[:], yt_ps[:], x_sb[:, bass.ds((c - 1) * CT, CT), :],
                                            ALU.add).then_inc(y_read, 1)
                    dve.wait_ge(y_read, c)
                    for t in range(CT):
                        last = nc.vector.bn_stats(stats4[:, t, :], z_sb[:, t, :])
                    last.then_inc(chain4, 1)
                    dve.wait_ge(chain4, link + 1)
                    nc.vector.memset(pause[:], 0.0)
                    for t in range(CT):
                        last = nc.vector.bn_aggr(mv4[:, t, :], stats4[:, t, :])
                    last.then_inc(chain4, 1)
                    dve.wait_ge(chain4, link + 2)
                    nc.vector.tensor_scalar(var_sb[:], mv4[:, :, 1], EPS, None, ALU.add).then_inc(var4, 1)

                def scale(pair, c, s):
                    link = (c - 1) * LINKS
                    dve.wait_ge(root4, c)
                    nc.vector.reciprocal(rstd_sb[:], root_sb[:]).then_inc(chain4, 1)
                    dve.wait_ge(chain4, link + 3)
                    if not isinstance(c, int) or c > 2:
                        dve.wait_ge(out_stored[0], pair * 16)
                    for t in range(CT):
                        last = nc.vector.tensor_scalar(out_sb[:, 1 - s, t, :], z_sb[:, t, :], mv4[:, t, 0:1],
                                                       rstd_sb[:, t:t + 1], ALU.subtract, ALU.mult)
                    last.then_inc(out_ready, 1)

                def chunk(pair, s, before, now):
                    c = pair * 2 + s
                    if not now:
                        finish(c, s)
                        scale(pair, c, s)
                        return
                    for e in range(E):
                        dve.wait_ge(h_used, c * HN + FC * (e + 1))
                        dve.wait_ge(gate_read, c * E + (e + 1))
                        if before or e >= 2:
                            dve.wait_ge(acc_added, c * E + (e - 1))
                        nc.vector.tensor_tensor(gated[:, e % 2, :], y_ps[:, e % 2, :], gate_sb[:, e % 2, :],
                                                ALU.mult).then_inc(y_gated, 1)
                        if e == 3 and before:
                            finish(c, s)
                        if e == 5 and before:
                            scale(pair, c, s)

                each_chunk(dve, chunk)

            @block.gpsimd
            def _(pool):
                def chunk(pair, s, before, now):
                    c = pair * 2 + s
                    if not now:
                        return
                    pool.wait_ge(acc_begun, c + 1)
                    for e in range(E):
                        pool.wait_ge(y_gated, c * E + (e + 1))
                        if before or e:
                            pool.wait_ge(acc_added, c * E + e)
                        nc.gpsimd.tensor_tensor(acc[:, s, :], acc[:, s, :], gated[:, e % 2, :],
                                                ALU.add).then_inc(acc_added, 1)

                each_chunk(pool, chunk)

            @block.sync
            def _(sp):
                for c in range(CHUNKS):
                    if c:
                        sp.wait_ge(out_stored[(c - 1) % 2], 16 * ((c + 1) // 2))
                    sp.wait_ge(out_ready, c + 1)
                    sp.dma_start(out[c * CT:(c + 1) * CT].rearrange("t p d -> p t d"),
                                 out_sb[:, c % 2]).then_inc(out_stored[c % 2], 16)
                for s in range(2):
                    sp.wait_ge(out_stored[s], 16 * (CHUNKS // 2))

        ffn.close()


def sinusoids():
    inv = np.float32(1.0) / np.float32(10000.0) ** (np.arange(0, D, 2, dtype=np.float32) / np.float32(D))
    ang = np.arange(-(L - 1), L, dtype=np.float32)[:, None] * inv[None, :].astype(np.float32)
    emb = np.zeros((2 * L - 1, D), np.float32)
    emb[:, 0::2] = np.sin(ang)
    emb[:, 1::2] = np.cos(ang)
    low = np.zeros((D, REL_PAD), np.float32)
    up = np.zeros((D, REL_PAD), np.float32)
    low[:, 0:L] = emb.T[:, L - 1:2 * L - 1]
    up[:, L + 1:2 * L - 1] = emb.T[:, 0:L - 2]
    return low, up


def kernel(L0_attn_w, L0_attn_Wq, L0_attn_Wk, L0_attn_Wv, L0_attn_Wr, L0_attn_u_bias, L0_attn_v_bias, L0_ffn_Wg,
           L0_ffn_bg, L0_ffn_W1, L0_ffn_b1, L0_ffn_W2, L0_ffn_b2):
    import concourse.bacc as bacc
    from concourse.bass_utils import run_bass_kernel_spmd

    w = np.asarray(L0_attn_w)
    low, up = sinusoids()
    sel = np.zeros((2 * E, E, P), np.float32)
    for e in range(E):
        sel[2 * e:2 * e + 2, e, :] = 1.0
    arrays = {
        "w_tok": w.reshape(B, NHI, HALF, LO, D).transpose(0, 2, 1, 3, 4).reshape(TILES, P, D),
        "wT": w.reshape(TOK, D).T,
        "WqT": np.asarray(L0_attn_Wq).T,
        "WkT": np.asarray(L0_attn_Wk).T,
        "WvT": np.asarray(L0_attn_Wv).T,
        "WrT": np.asarray(L0_attn_Wr).T,
        "u_bias": np.asarray(L0_attn_u_bias).reshape(D, 1),
        "v_bias": np.asarray(L0_attn_v_bias).reshape(D, 1),
        "sin_low": low,
        "sin_up": up,
        "ident_in": np.eye(P, dtype=np.float32),
        "earlier_in": np.tile(np.tril(np.ones((E, E), np.float32), -1).reshape(1, E * E), (P, 1)),
        "sel_in": sel,
        "Wg": np.asarray(L0_ffn_Wg),
        "bg": np.asarray(L0_ffn_bg),
        "W1": np.asarray(L0_ffn_W1),
        "b1T": np.asarray(L0_ffn_b1).reshape(HN, P).T,
        "W2": np.asarray(L0_ffn_W2),
        "b2": np.repeat(np.asarray(L0_ffn_b2), 2, axis=0),
    }
    arrays = {f"{n}_dram": np.ascontiguousarray(a) for n, a in arrays.items()}
    nc = bacc.Bacc("TRN2", target_bir_lowering=False, num_devices=1)
    args = [nc.dram_tensor(n, a.shape, F32, kind="ExternalInput").ap() for n, a in arrays.items()]
    out = nc.dram_tensor("out_dram", (TILES, P, D), F32, kind="ExternalOutput").ap()
    attention_moe_kernel(nc, *args, out)
    r = run_bass_kernel_spmd(nc, [arrays], core_ids=[0])
    y = r.results[0]["out_dram"]
    return y.reshape(B, HALF, NHI, LO, D).transpose(0, 2, 1, 3, 4).reshape(B, L, D)
```

```python
from contextlib import ExitStack

import numpy as np

import concourse.bass as bass
from concourse import mybir

F32 = mybir.dt.float32
F32R = mybir.dt.float32r
ALU = mybir.AluOpType
ACT = mybir.ActivationFunctionType
AX = mybir.AxisListType

P = 128
B, L, D = 16, 256, 128
H = 16
DH = D // H
E, F = 8, 512
FC = F // P
TOK = B * L
SCALE = 1.0 / float(np.sqrt(np.float32(DH)))
EPS = 1e-5

NHI = 8
HALF = 2
LO = 16
SHIFT = HALF * LO
NREL = L + SHIFT
REL_PAD = 2 * L
GB = 2
GS = 2 * GB
NG = B // GB
STEP_TILES = 4
UNIT_STEPS = LO // STEP_TILES
PAIR = 2
PAIRS = H // PAIR
PAIR_UNITS = PAIR * HALF
PAIR_STEPS = PAIR_UNITS * UNIT_STEPS
STEPS = PAIRS * PAIR_STEPS
VG = 4
VQ = B // VG
VE = DH + 1
VW = 32
PV_LAG = UNIT_STEPS + 1
OUT_LAG = PV_LAG + UNIT_STEPS
TAIL = PV_LAG + 1
POOL_LOADS = 9
TILES = TOK // P
CHUNK = 512
CHUNKS = TOK // CHUNK
CT = CHUNK // P
HN = E * FC


def attention_moe_kernel(nc, w_tok, wT, WqT, WkT, WvT, WrT, u_bias, v_bias, sin_low, sin_up, ident_in, order_in,
                         Wg, bg, W1, b1T, W2, b2, out):
    with ExitStack() as whole:
        def sem(name):
            return whole.enter_context(nc.semaphore(name))

        def alloc(stack, name, shape, dt=F32):
            return stack.enter_context(nc.sbuf_tensor(name, shape, dt))

        def psum(stack, name, shape):
            return stack.enter_context(nc.psum_tensor(name, shape, F32))

        q_rel_dram = nc.dram_tensor("q_rel_dram", [D, HALF, NHI, 2, B, 2, LO], F32).ap()
        q_key_dram = nc.dram_tensor("q_key_dram", [D, HALF, B, NHI, 2, LO], F32).ap()
        key_dram = nc.dram_tensor("key_dram", [D, B, 2 * L], F32).ap()
        rel_table = nc.dram_tensor("rel_dram", [D, 2, 2, REL_PAD], F32)
        rel_dram = rel_table.ap()
        rel_windows = bass.AP(rel_table, 0, [[DH * 4 * REL_PAD, H], [SHIFT, NHI], [REL_PAD, DH * 4], [1, NREL]])

        gate_dram = nc.dram_tensor("gate_dram", [E, TOK], F32).ap()

        attn = alloc(whole, "attn", [P, TILES, D])
        x_sb = alloc(whole, "x_sb", [P, TILES, D])
        ident = alloc(whole, "ident", [P, P])

        att = ExitStack()
        v_all = alloc(att, "v_all", [P, TILES, H, DH + 1])
        q_rel = alloc(att, "q_rel", [P, HALF, NHI, B, 2, LO], F32R)
        q_key = alloc(att, "q_key", [P, HALF, NHI, B, 2, LO], F32R)
        keys = alloc(att, "keys", [P, PAIR, 2, L], F32R)
        rel = alloc(att, "rel", [P, PAIR, 2, NREL], F32R)

        c_loaded = sem("c_loaded")
        wt_loaded = [sem(f"wt_loaded{i}") for i in range(4)]
        biases_scaled = sem("biases_scaled")
        rel_done = sem("rel_done")
        rel_high = sem("rel_high")
        rel_low = sem("rel_low")
        q_done = sem("q_done")
        k_done = sem("k_done")
        v_done = sem("v_done")
        q_full = sem("q_full")
        k_full = sem("k_full")
        v_copied = sem("v_copied")
        high_done = sem("high_done")
        low_done = sem("low_done")
        stored = [sem(f"stored{i}") for i in range(2)]
        q_stored = [sem(f"q_stored{i}") for i in range(2)]
        rel_stored = sem("rel_stored")
        C_LOADS = 9
        STORES = 2

        with ExitStack() as st:
            wT_sb = attn[:].rearrange("p t d -> p (t d)")
            wq_sb = alloc(st, "wq_sb", [P, D])
            wk_sb = alloc(st, "wk_sb", [P, D])
            wv_sb = alloc(st, "wv_sb", [P, D])
            wr_sb = alloc(st, "wr_sb", [P, D])
            sins = alloc(st, "sins", [P, 2, REL_PAD])
            bias = alloc(st, "bias", [P, 4])
            rel_stage = alloc(st, "rel_stage", [P, 2, 2, REL_PAD], F32R)
            full_v = alloc(st, "full_v", [P, 2, GB, L + SHIFT])
            full_u = alloc(st, "full_u", [P, 2, GB, L])
            full_k = alloc(st, "full_k", [P, 2, GB, L])
            stage_rel = alloc(st, "stage_rel", [P, 2, HALF, NHI, 2, GS, 2, LO], F32R)
            stage_q = alloc(st, "stage_q", [P, 2, HALF, GB, NHI, 2, LO], F32R)
            stage_k = alloc(st, "stage_k", [P, 2, GB, 2, L], F32R)
            rel_ps = psum(st, "rel_ps", [P, 2, REL_PAD])
            q_ps = psum(st, "q_ps", [P, 2, CHUNK])
            k_ps = psum(st, "k_ps", [P, 2, CHUNK])
            v_ps = psum(st, "v_ps", [P, 2, CT, D])
            block = st.enter_context(nc.Block())

            def rel_view(slot, up, half):
                start = half * LO + up
                return full_v[:, slot, :, start:start + L].rearrange("p b (h x) -> p h b x", x=SHIFT)[:, :, :, 0:LO]

            def stage_view(c, up, half, part):
                place = (c % 2) * GB
                return stage_rel[:, (c // 2) % 2, half, :, up, place:place + GB, part, :]

            def key_view(slot, half):
                return full_u[:, slot].rearrange("p b (h a l) -> p b h a l", h=NHI, a=HALF)[:, :, :, half, :]

            @block.sync
            def _(sp):
                sp.dma_start(wq_sb[:], WqT).then_inc(c_loaded, 16)
                sp.dma_start(bias[:, 0:1], u_bias).then_inc(c_loaded, 16)
                sp.dma_start(bias[:, 1:2], v_bias).then_inc(c_loaded, 16)
                sp.dma_start(wk_sb[:], WkT).then_inc(c_loaded, 16)
                sp.dma_start(wv_sb[:], WvT).then_inc(c_loaded, 16)
                sp.dma_start(wr_sb[:], WrT).then_inc(c_loaded, 16)
                sp.dma_start(sins[:, 0, :], sin_low).then_inc(c_loaded, 16)
                sp.dma_start(sins[:, 1, :], sin_up).then_inc(c_loaded, 16)
                sp.dma_start(ident[:], ident_in).then_inc(c_loaded, 16)
                for c in range(4):
                    part = slice(c * 1024, (c + 1) * 1024)
                    sp.dma_start(wT_sb[:, part], wT[:, part]).then_inc(wt_loaded[c], 16)
                sp.wait_ge(rel_low, 1)
                sp.dma_start(rel_dram.rearrange("p a b x -> p (a b x)"),
                             rel_stage[:].bitcast(F32).rearrange("p a b x -> p (a b x)")).then_inc(rel_stored, 16)
                for c in range(NG):
                    slot = c % 2
                    sp.wait_ge(high_done, c + 1)
                    sp.wait_ge(low_done, c + 1)
                    sp.dma_start(
                        q_key_dram[:, :, c * GB:(c + 1) * GB].rearrange("p a b h t x -> p a (b h t x)"),
                        stage_q[:, slot].bitcast(F32).rearrange("p a b h t x -> p a (b h t x)")).then_inc(
                            stored[slot], 16)
                    sp.dma_start(
                        key_dram[:, c * GB:(c + 1) * GB, :].rearrange("p b x -> p (b x)"),
                        stage_k[:, slot].bitcast(F32).rearrange("p b l x -> p (b l x)")).then_inc(stored[slot], 16)
                    if c % 2 == 1:
                        first = (c - 1) * GB
                        sp.dma_start(
                            q_rel_dram[:, :, :, :, first:first + GS].rearrange("p a h u b t x -> p (a h u) (b t x)"),
                            stage_rel[:, (c // 2) % 2].bitcast(F32).rearrange(
                                "p a h u b t x -> p (a h u) (b t x)")).then_inc(q_stored[(c // 2) % 2], 16)
                for slot in range(2):
                    sp.wait_ge(stored[slot], 16 * STORES * (NG // 2))
                    sp.wait_ge(q_stored[slot], 16 * (NG // 4))
                sp.wait_ge(rel_stored, 16)

            @block.tensor
            def _(pe):
                pe.wait_ge(c_loaded, 16 * C_LOADS)
                for c in range(NG):
                    slot = c % 2
                    if c % 2 == 0:
                        pe.wait_ge(wt_loaded[c // 2], 16)
                    cols = wT_sb[:, c * CHUNK:(c + 1) * CHUNK]
                    if c >= 2:
                        pe.wait_ge(q_full, c - 1)
                    nc.tensor.matmul(q_ps[:, slot, :], wq_sb[:], cols, start=True, stop=True).then_inc(q_done, 1)
                    if c >= 2:
                        pe.wait_ge(k_full, c - 1)
                    nc.tensor.matmul(k_ps[:, slot, :], wk_sb[:], cols, start=True, stop=True).then_inc(k_done, 1)
                    if c >= 2:
                        pe.wait_ge(v_copied, c - 1)
                    for t in range(CT):
                        last = nc.tensor.matmul(v_ps[:, slot, t, :], cols[:, t * P:(t + 1) * P], wv_sb[:],
                                                start=True, stop=True)
                    last.then_inc(v_done, 1)
                    if c == 0:
                        for up in range(2):
                            last = nc.tensor.matmul(rel_ps[:, up, :], wr_sb[:], sins[:, up, :], start=True, stop=True)
                        last.then_inc(rel_done, 1)

            @block.scalar
            def _(act):
                act.wait_ge(biases_scaled, 1)
                for c in range(NG):
                    slot = c % 2
                    if c >= 2:
                        act.wait_ge(low_done, c - 1)
                        act.wait_ge(stored[slot], 16 * STORES * (c // 2))
                    if c >= 4:
                        act.wait_ge(q_stored[(c // 2) % 2], 16 * (c // 4))
                    act.wait_ge(q_done, c + 1)
                    src = q_ps[:, slot, :].rearrange("p (b i) -> p b i", b=GB)
                    nc.scalar.activation(full_u[:, slot], src, ACT.Identity, bias=bias[:, 2:3], scale=SCALE)
                    nc.scalar.activation(full_v[:, slot, :, 0:L], src, ACT.Identity,
                                         bias=bias[:, 3:4], scale=SCALE).then_inc(q_full, 1)
                    act.wait_ge(k_done, c + 1)
                    nc.scalar.copy(full_k[:, slot], k_ps[:, slot, :].rearrange("p (b i) -> p b i", b=GB)).then_inc(
                        k_full, 1)
                    act.wait_ge(q_full, c + 1)
                    act.wait_ge(k_full, c + 1)
                    for up in range(2):
                        for half in range(HALF):
                            nc.scalar.copy(stage_view(c, up, half, 0), rel_view(slot, up, half))
                    for half in range(HALF):
                        nc.scalar.copy(stage_q[:, slot, half, :, :, 0, :], key_view(slot, half))
                    nc.scalar.copy(stage_k[:, slot, :, 0, :], full_k[:, slot]).then_inc(high_done, 1)
                    if c == 0:
                        act.wait_ge(rel_done, 1)
                        nc.scalar.copy(rel_stage[:, :, 0, :], rel_ps[:]).then_inc(rel_high, 1)

            @block.vector
            def _(dve):
                nc.vector.memset(full_v[:, :, :, L:L + SHIFT], 0.0)
                nc.vector.memset(v_all[:, :, :, DH:DH + 1], 1.0)
                dve.wait_ge(c_loaded, 16 * C_LOADS)
                nc.vector.tensor_scalar(bias[:, 2:4], bias[:, 0:2], SCALE, None, ALU.mult).then_inc(biases_scaled, 1)
                for c in range(NG):
                    slot = c % 2
                    dve.wait_ge(v_done, c + 1)
                    nc.vector.tensor_copy(v_all[:, CT * c:CT * (c + 1), :, 0:DH],
                                          v_ps[:, slot].rearrange("p t (h d) -> p t h d", h=H)).then_inc(v_copied, 1)
                    dve.wait_ge(high_done, c + 1)
                    for up in range(2):
                        for half in range(HALF):
                            low, high = [stage_view(c, up, half, part) for part in (1, 0)]
                            nc.vector.tensor_tensor(low, rel_view(slot, up, half), high.bitcast(F32), ALU.subtract)
                    for half in range(HALF):
                        low, high = [stage_q[:, slot, half, :, :, part, :] for part in (1, 0)]
                        nc.vector.tensor_tensor(low, key_view(slot, half), high.bitcast(F32), ALU.subtract)
                    nc.vector.tensor_tensor(stage_k[:, slot, :, 1, :], full_k[:, slot],
                                            stage_k[:, slot, :, 0, :].bitcast(F32),
                                            ALU.subtract).then_inc(low_done, 1)
                    if c == 0:
                        dve.wait_ge(rel_high, 1)
                        nc.vector.tensor_tensor(rel_stage[:, :, 1, :], rel_ps[:],
                                                rel_stage[:, :, 0, :].bitcast(F32),
                                                ALU.subtract).then_inc(rel_low, 1)

            @block.gpsimd
            def _(pool):
                nc.gpsimd.memset(q_rel[:].bitcast(F32), 0.0)
                nc.gpsimd.memset(q_key[:].bitcast(F32), 0.0)

        q_loaded = [sem(f"q_loaded{i}") for i in range(HALF)]
        head_loaded = [sem(f"head_loaded{i}") for i in range(PAIR)]
        first_content = sem("first_content")
        x_loaded = sem("x_loaded")
        scores_done = sem("scores_done")
        max_done = sem("max_done")
        exp_done = sem("exp_done")
        turned = sem("turned")
        pv_done = sem("pv_done")
        o_copied = sem("o_copied")
        o_turned = sem("o_turned")
        recip_done = sem("recip_done")
        o_scaled = sem("o_scaled")
        v_padded = sem("v_padded")
        v_high = sem("v_high")
        v_ready = sem("v_ready")
        turned_high = sem("turned_high")
        turned_low = sem("turned_low")
        low_moved = sem("low_moved")
        summed = sem("summed")
        Q_LOADED = 16 * (NHI + B)
        HEAD_LOADED = 16 * 2

        with ExitStack() as st:
            probsT = alloc(st, "probsT", [P, 2, 2, 2, NHI, B, LO], F32R)
            probs = alloc(st, "probs", [P, 2, STEP_TILES, L])
            v_head = alloc(st, "v_head", [P, PAIR, TILES, VW], F32R)
            v_full = alloc(st, "v_full", [P, TILES, VE])
            o_sb = alloc(st, "o_sb", [VG * VW, P])
            neg_max = alloc(st, "neg_max", [P, 2, STEP_TILES])
            low_sums = alloc(st, "low_sums", [P, B, VE])
            sums = alloc(st, "sums", [P, B, VE])
            recip = alloc(st, "recip", [P, B])
            s_ps = psum(st, "s_ps", [P, 2, STEP_TILES, L])
            t_ps = psum(st, "t_ps", [P, 2, 2, 2, P])
            o_ps = psum(st, "o_ps", [VW, VG, P])
            ot_ps = psum(st, "ot_ps", [P, B, VW])
            block = st.enter_context(nc.Block())

            def each_step(eng, step):
                for k in range(PAIR_STEPS):
                    step(0, k, k)
                with eng.Fori(1, PAIRS) as pair:
                    for k in range(PAIR_STEPS):
                        step(pair, k, PAIR_STEPS + k)
                for k in range(TAIL):
                    step(PAIRS, k, STEPS + k)

            def turned_views(unit, v, c):
                lo = (v % UNIT_STEPS) * STEP_TILES + 2 * c
                return [probsT[:, unit % 2, part, :, :, :, lo:lo + 2].rearrange("p j h b t -> p t j (h b)")
                        for part in range(2)]

            def load_content(eng, rows, half, batches, loaded):
                for b in batches:
                    eng.dma_start(
                        q_key[b * DH:(b + 1) * DH, half, :, b].bitcast(F32).rearrange("p h t x -> p h (t x)"),
                        q_key_dram[rows, half, b].rearrange("d h t x -> d h (t x)")).then_inc(loaded, 16)

            @block.sync
            def _(sp):
                def load_pair(pair, first):
                    for k in range(PAIR_UNITS):
                        hd = k // HALF
                        half = k % HALF
                        rows = bass.ds(pair * (PAIR * DH) + hd * DH, DH)
                        if not (first and k < 2):
                            sp.wait_ge(scores_done, pair * PAIR_STEPS + (k - 1) * UNIT_STEPS)
                        if half == 0:
                            sp.dma_start(
                                keys[:, hd].bitcast(F32).rearrange("p a x -> p (a x)"),
                                key_dram[rows].rearrange("d b x -> b d x")).then_inc(head_loaded[hd], 16)
                            sp.dma_start(
                                rel[:, hd].bitcast(F32).rearrange("p a x -> p (a x)"),
                                rel_windows[bass.ds(pair * PAIR + hd, 1)].rearrange("o g r x -> (o g) r x")).then_inc(
                                    head_loaded[hd], 16)
                        for hi in range(NHI):
                            r = (NHI - 1 - hi) * 2 * DH
                            sp.dma_start(
                                q_rel[r:r + 2 * DH, half, hi].bitcast(F32).rearrange("p b t x -> p (b t x)"),
                                q_rel_dram[rows, half, hi].rearrange("d u b t x -> d u (b t x)")).then_inc(
                                    q_loaded[half], 16)
                        load_content(sp, rows, half, range(B - POOL_LOADS if first and k == 0 else B), q_loaded[half])

                load_pair(0, True)
                sp.dma_start(x_sb[:], w_tok.rearrange("t p d -> p t d")).then_inc(x_loaded, 16)
                with sp.Fori(1, PAIRS) as pair:
                    load_pair(pair, False)

            @block.gpsimd
            def _(pool):
                load_content(pool, slice(0, DH), 0, range(B - POOL_LOADS, B), first_content)
                nc.gpsimd.memset(v_head[:].bitcast(F32), 0.0).then_inc(v_padded, 1)
                pool.wait_ge(v_padded, 1)

                def values(pair, first):
                    for hd in range(PAIR):
                        if not first:
                            pool.wait_ge(pv_done, pair * PAIR_STEPS + (hd - 1) * HALF * UNIT_STEPS)
                        if not (first and hd == 0):
                            pool.wait_ge(v_ready, pair * PAIR + hd)
                        full = v_all[:, :, bass.ds(pair * PAIR + hd, 1), :].rearrange("p t h d -> p t (h d)")
                        nc.gpsimd.tensor_copy(v_head[:, hd, :, 0:VE], full)
                        nc.gpsimd.tensor_copy(v_full[:], full).then_inc(v_high, 1)
                        pool.wait_ge(v_high, pair * PAIR + (hd + 1))
                        nc.gpsimd.tensor_tensor(v_head[:, hd, :, VE:2 * VE], v_full[:],
                                                v_head[:, hd, :, 0:VE].bitcast(F32),
                                                ALU.subtract).then_inc(v_ready, 1)

                values(0, True)
                with pool.Fori(1, PAIRS) as pair:
                    values(pair, False)

            @block.tensor
            def _(pe):
                def scores(pair, k, at):
                    unit = k // UNIT_STEPS
                    half = unit % HALF
                    hd = unit // HALF
                    if k % UNIT_STEPS == 0:
                        other_queue = 16 * POOL_LOADS if half == 0 else 0
                        pe.wait_ge(q_loaded[half],
                                   pair * (PAIR * Q_LOADED) + ((unit // HALF + 1) * Q_LOADED - other_queue))
                        if at == 0:
                            pe.wait_ge(first_content, 16 * POOL_LOADS)
                        if half == 0:
                            pe.wait_ge(head_loaded[hd], pair * HEAD_LOADED + HEAD_LOADED)
                    if at >= 2:
                        pe.wait_ge(exp_done, pair * PAIR_STEPS + (k - 1))
                    for t in range(STEP_TILES):
                        lo = (k % UNIT_STEPS) * STEP_TILES + t
                        start = SHIFT - 1 - (half * LO + lo)
                        q_r = [q_rel[:, half, :, :, x, lo].rearrange("p h b -> p (h b)") for x in range(2)]
                        r = [rel[:, hd, x, start:start + L] for x in range(2)]
                        q_k = [q_key[:, half, :, :, x, lo].rearrange("p h b -> p (h b)") for x in range(2)]
                        ks = [keys[:, hd, x, :] for x in range(2)]
                        o = s_ps[:, k % 2, t, :]
                        nc.tensor.matmul(o, q_r[0], r[0], start=True, stop=False)
                        nc.tensor.matmul(o, q_r[0], r[1], start=False, stop=False)
                        nc.tensor.matmul(o, q_r[1], r[0], start=False, stop=False)
                        nc.tensor.matmul(o, q_k[0], ks[0], start=False, stop=False)
                        nc.tensor.matmul(o, q_k[0], ks[1], start=False, stop=False)
                        last = nc.tensor.matmul(o, q_k[1], ks[0], start=False, stop=True)
                    last.then_inc(scores_done, 1)

                def turn_out(pair, k, at):
                    v = k - PV_LAG - 1
                    q = v % UNIT_STEPS
                    pe.wait_ge(o_copied, pair * PAIR_STEPS + (v + 1))
                    if q == 0 and at > PV_LAG + UNIT_STEPS:
                        pe.wait_ge(summed, pair * PAIR_UNITS + v // UNIT_STEPS)

                    nc.tensor.transpose(ot_ps[:, q * VG:(q + 1) * VG, :].rearrange("p g x -> p (g x)"), o_sb[:],
                                        ident[:]).then_inc(o_turned, 1)

                def values(pair, k, at):
                    v = k - PV_LAG
                    q = v % UNIT_STEPS
                    unit = v // UNIT_STEPS
                    hd = (unit // HALF) % PAIR
                    if q == 0:
                        pe.wait_ge(turned_low, pair * (2 * PAIR_STEPS) + 2 * (v + UNIT_STEPS))
                        pe.wait_ge(v_ready, pair * PAIR + (unit // HALF + 1))
                    if at > PV_LAG:
                        pe.wait_ge(o_copied, pair * PAIR_STEPS + v)
                    for g in range(VG):
                        b = q * VG + g
                        for n in range(4):
                            part, jh = n // 2, n % 2
                            last = nc.tensor.matmul(o_ps[:, g, :], v_head[:, hd, 2 * b + jh, :],
                                                    probsT[:, unit % 2, part, jh, :, b, :], start=n == 0, stop=n == 3)
                    last.then_inc(pv_done, 1)

                def turn_probs(pair, k, at):
                    pe.wait_ge(exp_done, pair * PAIR_STEPS + k)
                    for c in range(2):
                        if at >= 2:
                            pe.wait_ge(turned_low, pair * (2 * PAIR_STEPS) + (2 * (k - 1) + c - 1))
                        for t in range(2):
                            for jh in range(2):
                                last = nc.tensor.transpose(t_ps[:, c, t, jh, :],
                                                           probs[:, (k - 1) % 2, 2 * c + t, jh * P:(jh + 1) * P],
                                                           ident[:])
                        last.then_inc(turned, 1)

                def step(pair, k, at):
                    if at < STEPS:
                        scores(pair, k, at)
                    if 1 <= at <= STEPS:
                        turn_probs(pair, k, at)
                    if PV_LAG < at <= STEPS + PV_LAG:
                        turn_out(pair, k, at)
                    if PV_LAG <= at < STEPS + PV_LAG:
                        values(pair, k, at)

                each_step(pe, step)

            @block.vector
            def _(dve):
                def low_parts(pair, k, c):
                    v = k - 1
                    dve.wait_ge(turned_high, pair * (2 * PAIR_STEPS) + (2 * v + c + 1))
                    high, low = turned_views(v // UNIT_STEPS, v, c)
                    nc.vector.tensor_tensor(low, t_ps[:, c], high.bitcast(F32), ALU.subtract).then_inc(turned_low, 1)

                def step(pair, k, at):
                    if at < STEPS:
                        dve.wait_ge(scores_done, pair * PAIR_STEPS + (k + 1))
                        nc.vector.tensor_reduce(neg_max[:, k % 2, :], s_ps[:, k % 2], axis=AX.X, op=ALU.max,
                                                negate=True).then_inc(max_done, 1)
                    if 1 <= at <= STEPS:
                        for c in range(2):
                            low_parts(pair, k, c)
                    if PV_LAG <= at < STEPS + PV_LAG:
                        v = k - PV_LAG
                        dve.wait_ge(pv_done, pair * PAIR_STEPS + (v + 1))
                        if at > PV_LAG:
                            dve.wait_ge(o_turned, pair * PAIR_STEPS + v)
                        for g in range(VG):
                            last = nc.vector.tensor_copy(o_sb[g * VW:(g + 1) * VW, :], o_ps[:, g, :])
                        last.then_inc(o_copied, 1)
                    out = at >= OUT_LAG and (k - OUT_LAG) % UNIT_STEPS == 0
                    n = (k - OUT_LAG) // UNIT_STEPS
                    if out:
                        dve.wait_ge(o_turned, pair * PAIR_STEPS + (n + 1) * UNIT_STEPS)
                        nc.vector.tensor_copy(low_sums[:], ot_ps[:, :, VE:2 * VE]).then_inc(low_moved, 1)
                        dve.wait_ge(low_moved, pair * PAIR_UNITS + (n + 1))
                        nc.vector.tensor_tensor(sums[:], ot_ps[:, :, 0:VE], low_sums[:], ALU.add).then_inc(summed, 1)
                        dve.wait_ge(summed, pair * PAIR_UNITS + (n + 1))
                        nc.vector.reciprocal(recip[:], sums[:, :, DH]).then_inc(recip_done, 1)
                        dve.wait_ge(recip_done, pair * PAIR_UNITS + (n + 1))
                        head_cols = bass.ds(pair * (PAIR * DH) + (n // HALF) * DH, DH)
                        dst = attn[:].rearrange("p (b a) d -> p b a d", a=HALF)[:, :, n % HALF, head_cols]
                        nc.vector.tensor_tensor(dst, sums[:, :, 0:DH], recip[:].unsqueeze(2).to_broadcast([P, B, DH]),
                                                ALU.mult).then_inc(o_scaled, 1)

                each_step(dve, step)

            @block.scalar
            def _(act):
                def step(pair, k, at):
                    if 1 <= at <= STEPS:
                        v = k - 1
                        unit = v // UNIT_STEPS
                        for c in range(2):
                            if v % UNIT_STEPS == 0 and c == 0 and at > 2 * UNIT_STEPS:
                                act.wait_ge(pv_done, pair * PAIR_STEPS + (unit - 1) * UNIT_STEPS)
                            act.wait_ge(turned, pair * (2 * PAIR_STEPS) + (2 * v + c + 1))
                            high, low = turned_views(unit, v, c)
                            nc.scalar.copy(high, t_ps[:, c]).then_inc(turned_high, 1)
                    if at < STEPS:
                        act.wait_ge(max_done, pair * PAIR_STEPS + (k + 1))
                        if at >= 2:
                            act.wait_ge(turned, pair * (2 * PAIR_STEPS) + 2 * (k - 1))
                        for t in range(STEP_TILES):
                            last = nc.scalar.activation(probs[:, k % 2, t, :], s_ps[:, k % 2, t, :], ACT.Exp,
                                                        bias=neg_max[:, k % 2, t:t + 1], scale=1.0)
                        last.then_inc(exp_done, 1)

                each_step(act, step)

        att.close()

        more_loaded = sem("more_loaded")
        chain = sem("chain")
        var_ready = sem("var_ready")
        root_done = sem("root_done")
        normed = sem("normed")
        x_turned = sem("x_turned")
        x_high = sem("x_high")
        x_low = sem("x_low")
        x_copied = sem("x_copied")
        residual_added = sem("residual_added")
        w1_loaded = sem("w1_loaded")
        w_high = sem("w_high")
        w2_loaded = sem("w2_loaded")
        logits_done = sem("logits_done")
        shifted = sem("shifted")
        exp_gates = sem("exp_gates")
        gates_done = sem("gates_done")
        g_turned = sem("g_turned")
        g_copied = [sem(f"g_copied{i}") for i in range(2)]
        first_stored = sem("first_stored")
        g_stored = sem("g_stored")
        gates_spread = [sem(f"gates_spread{i}") for i in range(2)]
        MORE = 5

        ffn = ExitStack()
        w2h = alloc(ffn, "w2h", [P, E, FC, D], F32R)
        w2l = alloc(ffn, "w2l", [P, E, FC, D], F32R)
        w1h = alloc(ffn, "w1h", [P, E, F], F32R)
        w1l = alloc(ffn, "w1l", [P, E, F], F32R)
        b1_sb = alloc(ffn, "b1_sb", [P, HN])
        xh = alloc(ffn, "xh", [P, TOK], F32R)
        xl = alloc(ffn, "xl", [P, TOK], F32R)
        gT = alloc(ffn, "gT", [E, TOK])
        b2_sb = alloc(ffn, "b2_sb", [E, D])
        HE = E // 2
        gate_sb = attn[:].rearrange("p (u e a) d -> p u e (a d)", u=2, e=HE)

        def spread_gates(sp, c, half):
            cols = gate_dram[half * HE:(half + 1) * HE, c * CHUNK:(c + 1) * CHUNK]
            sp.dma_start(gate_sb[:, half], cols.partition_broadcast(P)).then_inc(gates_spread[half], 16)

        with ExitStack() as st:
            w1_sb = alloc(st, "w1_sb", [P, E, F])
            w2_sb = alloc(st, "w2_sb", [P, E, FC, D])
            wg_sb = alloc(st, "wg_sb", [P, E])
            bg_sb = alloc(st, "bg_sb", [P, E])
            order = alloc(st, "order", [P, E])
            stats = alloc(st, "stats", [P, TILES, 6])
            mv = alloc(st, "mv", [P, TILES, 2])
            var = alloc(st, "var", [P, TILES])
            root = alloc(st, "root", [P, TILES])
            rstd = alloc(st, "rstd", [P, TILES])
            xfull = alloc(st, "xfull", [P, 2, CT, P])
            logit = alloc(st, "logit", [P, TILES, E])
            gate = alloc(st, "gate", [P, TILES, E])
            red = alloc(st, "red", [P, TILES])
            rest = alloc(st, "rest", [P, TILES, E])
            keep = alloc(st, "keep", [P, TILES, E])
            picked = alloc(st, "picked", [P, 2, TILES, E])
            place = alloc(st, "place", [P, TILES, E])
            xt_ps = psum(st, "xt_ps", [P, 4, CT, P])
            l_ps = psum(st, "l_ps", [P, 512])
            g_ps = psum(st, "g_ps", [E, 2, CHUNK])
            weights = [(w1l[:, e], w1_sb[:, e], w1h[:, e]) for e in range(E)]
            weights += [(w2l[:, e], w2_sb[:, e], w2h[:, e]) for e in range(E)]
            block = st.enter_context(nc.Block())

            @block.sync
            def _(sp):
                sp.wait_ge(x_loaded, 16)
                sp.dma_start(wg_sb[:], Wg).then_inc(more_loaded, 16)
                sp.dma_start(bg_sb[:], bg.partition_broadcast(P)).then_inc(more_loaded, 16)
                sp.dma_start(order[:], order_in).then_inc(more_loaded, 16)
                sp.dma_start(b1_sb[:], b1T).then_inc(more_loaded, 16)
                sp.dma_start(b2_sb[:], b2).then_inc(more_loaded, 16)
                sp.dma_start(w1_sb[:], W1.rearrange("e d f -> d e f")).then_inc(w1_loaded, 16)
                sp.dma_start(w2_sb[:], W2.rearrange("e (c p) d -> p e c d", p=P)).then_inc(w2_loaded, 16)
                sp.wait_ge(g_copied[0], 1)
                sp.dma_start(gate_dram[:, 0:CHUNK], gT[:, 0:CHUNK]).then_inc(first_stored, 16)
                sp.wait_ge(first_stored, 16)
                for half in range(2):
                    spread_gates(sp, 0, half)
                for part in range(2):
                    sp.wait_ge(g_copied[part], CHUNKS // 2)
                sp.dma_start(gate_dram[:, CHUNK:TOK], gT[:, CHUNK:TOK]).then_inc(g_stored, 16)

            @block.gpsimd
            def _(pool):
                pool.wait_ge(x_loaded, 16)
                for c in range(CHUNKS):
                    tiles = slice(c * CT, (c + 1) * CT)
                    nc.gpsimd.tensor_tensor(attn[:, tiles, :], attn[:, tiles, :], x_sb[:, tiles, :],
                                            ALU.add).then_inc(residual_added, 1)
                for n, (low, raw, high) in enumerate(weights):
                    pool.wait_ge(w_high, n + 1)
                    nc.gpsimd.tensor_tensor(low, raw, high.bitcast(F32), ALU.subtract)

            @block.vector
            def _(dve):
                links = [0]

                def link(ins):
                    links[0] += 1
                    ins.then_inc(chain, 1)
                    dve.wait_ge(chain, links[0])

                def spread(row):
                    return row.unsqueeze(2).to_broadcast([P, TILES, E])

                def moments(c):
                    tiles = slice(c * CT, (c + 1) * CT)
                    dve.wait_ge(residual_added, c + 1)
                    for t in range(c * CT, (c + 1) * CT):
                        last = nc.vector.bn_stats(stats[:, t, :], attn[:, t, :])
                    link(last)
                    for t in range(c * CT, (c + 1) * CT):
                        last = nc.vector.bn_aggr(mv[:, t, :], stats[:, t, :])
                    link(last)
                    nc.vector.tensor_scalar(var[:, tiles], mv[:, tiles, 1], EPS, None, ALU.add).then_inc(var_ready, 1)

                def normalise(c):
                    tiles = slice(c * CT, (c + 1) * CT)
                    dve.wait_ge(root_done, c + 1)
                    link(nc.vector.reciprocal(rstd[:, tiles], root[:, tiles]))
                    for t in range(c * CT, (c + 1) * CT):
                        last = nc.vector.tensor_scalar(x_sb[:, t, :], attn[:, t, :], mv[:, t, 0:1], rstd[:, t:t + 1],
                                                       ALU.subtract, ALU.mult)
                    last.then_inc(normed, 1)

                def low_part(c):
                    dve.wait_ge(x_high, c + 1)
                    dve.wait_ge(x_copied, c + 1)
                    cols = slice(c * CHUNK, (c + 1) * CHUNK)
                    nc.vector.tensor_tensor(xl[:, cols], xfull[:, c % 2].rearrange("p a b -> p (a b)"),
                                            xh[:, cols].bitcast(F32), ALU.subtract).then_inc(x_low, 1)

                for c in range(CHUNKS + 2):
                    if c < CHUNKS:
                        moments(c)
                    if 1 <= c <= CHUNKS:
                        normalise(c - 1)
                    if c >= 2:
                        low_part(c - 2)
                dve.wait_ge(more_loaded, 16 * MORE)
                dve.wait_ge(logits_done, CHUNKS)
                link(nc.vector.tensor_tensor(logit[:], l_ps[:, 0:TILES * E].rearrange("p (t e) -> p t e", e=E),
                                             bg_sb[:].unsqueeze(1).to_broadcast([P, TILES, E]), ALU.add))
                link(nc.vector.tensor_reduce(red[:], logit[:], axis=AX.X, op=ALU.max))
                nc.vector.tensor_tensor(logit[:], logit[:], spread(red[:]), ALU.subtract).then_inc(shifted, 1)
                dve.wait_ge(exp_gates, 1)
                link(nc.vector.tensor_reduce(red[:], gate[:], axis=AX.X, op=ALU.add))
                link(nc.vector.reciprocal(red[:], red[:]))
                link(nc.vector.tensor_tensor(gate[:], gate[:], spread(red[:]), ALU.mult))
                for n in range(2):
                    source = rest if n else gate
                    link(nc.vector.tensor_reduce(red[:], source[:], axis=AX.X, op=ALU.max))
                    link(nc.vector.tensor_tensor(place[:], source[:], spread(red[:]), ALU.is_equal))
                    link(nc.vector.scalar_tensor_tensor(place[:], place[:], -float(E),
                                                        order[:].unsqueeze(1).to_broadcast([P, TILES, E]),
                                                        ALU.mult, ALU.add))
                    link(nc.vector.tensor_reduce(red[:], place[:], axis=AX.X, op=ALU.min))
                    link(nc.vector.tensor_tensor(picked[:, n], place[:], spread(red[:]), ALU.is_equal))
                    if n == 0:
                        link(nc.vector.scalar_tensor_tensor(rest[:], picked[:, 0], -2.0, gate[:], ALU.mult, ALU.add))
                link(nc.vector.tensor_tensor(keep[:], picked[:, 0], picked[:, 1], ALU.add))
                nc.vector.tensor_tensor(gate[:], gate[:], keep[:], ALU.mult).then_inc(gates_done, 1)
                for c in range(1, CHUNKS, 2):
                    dve.wait_ge(g_turned, c + 1)
                    nc.vector.tensor_copy(gT[:, c * CHUNK:(c + 1) * CHUNK], g_ps[:, 1, :]).then_inc(g_copied[1], 1)

            @block.scalar
            def _(act):
                def take_root(c):
                    act.wait_ge(var_ready, c + 1)
                    tiles = slice(c * CT, (c + 1) * CT)
                    nc.scalar.activation(root[:, tiles], var[:, tiles], ACT.Sqrt).then_inc(root_done, 1)

                def high_parts(first, last):
                    for n in range(first, last):
                        if n % E == 0:
                            act.wait_ge(w2_loaded if n else w1_loaded, 16)
                        low, raw, high = weights[n]
                        nc.scalar.copy(high, raw).then_inc(w_high, 1)

                for c in range(2):
                    take_root(c)
                for c in range(CHUNKS):
                    if c + 2 < CHUNKS:
                        take_root(c + 2)
                    act.wait_ge(x_turned, c + 1)
                    if c >= 2:
                        act.wait_ge(logits_done, c - 1)
                        act.wait_ge(x_low, c - 1)
                    nc.scalar.copy(xh[:, c * CHUNK:(c + 1) * CHUNK],
                                   xt_ps[:, c % 4].rearrange("p a b -> p (a b)")).then_inc(x_high, 1)
                    nc.scalar.copy(xfull[:, c % 2], xt_ps[:, c % 4]).then_inc(x_copied, 1)
                    if c >= 2:
                        high_parts(3 * (c - 2), min(3 * (c - 1), 2 * E))
                act.wait_ge(shifted, 1)
                nc.scalar.activation(gate[:], logit[:], ACT.Exp).then_inc(exp_gates, 1)
                for c in range(0, CHUNKS, 2):
                    act.wait_ge(g_turned, c + 1)
                    nc.scalar.copy(gT[:, c * CHUNK:(c + 1) * CHUNK], g_ps[:, 0, :]).then_inc(g_copied[0], 1)

            @block.tensor
            def _(pe):
                def logits(c):
                    pe.wait_ge(x_copied, c + 1)
                    for t in range(CT):
                        n = c * CT + t
                        last = nc.tensor.matmul(l_ps[:, n * E:(n + 1) * E], xfull[:, c % 2, t, :], wg_sb[:],
                                                start=True, stop=True)
                    last.then_inc(logits_done, 1)

                pe.wait_ge(more_loaded, 16 * MORE)
                for c in range(CHUNKS):
                    pe.wait_ge(normed, c + 1)
                    if c >= 4:
                        pe.wait_ge(x_high, c - 3)
                        pe.wait_ge(x_copied, c - 3)
                    for t in range(CT):
                        last = nc.tensor.transpose(xt_ps[:, c % 4, t, :], x_sb[:, CT * c + t, :], ident[:])
                    last.then_inc(x_turned, 1)
                    if c:
                        logits(c - 1)
                logits(CHUNKS - 1)
                pe.wait_ge(gates_done, 1)
                for c in range(CHUNKS):
                    if c >= 2:
                        pe.wait_ge(g_copied[c % 2], c // 2)
                    for t in range(CT):
                        last = nc.tensor.transpose(g_ps[:, c % 2, t * P:(t + 1) * P],
                                                   gate[:, CT * c + t, :], ident[:])
                    last.then_inc(g_turned, 1)

        h_done = sem("h_done")
        h_gated = sem("h_gated")
        h_relu_done = sem("h_relu_done")
        h_low_done = sem("h_low_done")
        h_used = sem("h_used")
        y_copied = sem("y_copied")
        y_turned = sem("y_turned")
        y_read = sem("y_read")
        chain4 = sem("chain4")
        var4 = sem("var4")
        root4 = sem("root4")
        out_ready = sem("out_ready")
        out_stored = [sem(f"out_stored{i}") for i in range(2)]
        LAGH = 3
        COPY_AT = 4
        TURN_AT = 8
        NORM_AT = 10
        VAR_AT = 13
        ROOT_AT = 16
        SCALE_AT = (19, 22)
        LINKS = 3

        with ExitStack() as st:
            h_sb = alloc(st, "h_sb", [P, 4, CHUNK])
            h_full = alloc(st, "h_full", [P, 2, CHUNK])
            h_high = alloc(st, "h_high", [P, 4, CHUNK], F32R)
            h_low = alloc(st, "h_low", [P, 4, CHUNK], F32R)
            y_sb = alloc(st, "y_sb", [P, CHUNK])
            z_sb = alloc(st, "z_sb", [P, CT, D])
            out_sb = alloc(st, "out_sb", [P, 2, CT, D])
            stats4 = alloc(st, "stats4", [P, CT, 6])
            mv4 = alloc(st, "mv4", [P, CT, 2])
            var_sb = alloc(st, "var_sb", [P, CT])
            root_sb = alloc(st, "root_sb", [P, CT])
            rstd_sb = alloc(st, "rstd_sb", [P, CT])
            pause = alloc(st, "pause", [P, 1])
            h_ps = psum(st, "h_ps", [P, 4, CHUNK])
            y_ps = psum(st, "y_ps", [P, 2, CHUNK])
            yt_ps = psum(st, "yt_ps", [P, CT, P])
            block = st.enter_context(nc.Block())

            def each_chunk(eng, chunk):
                for s in range(2):
                    chunk(0, s, s > 0, True)
                with eng.Fori(1, CHUNKS // 2) as pair:
                    for s in range(2):
                        chunk(pair, s, True, True)
                chunk(CHUNKS // 2, 0, True, False)

            @block.tensor
            def _(pe):
                def chunk(pair, s, before, now):
                    c = pair * 2 + s
                    cols = bass.ds(c * CHUNK, CHUNK)
                    for n in range(HN):
                        if now:
                            e = n // FC
                            part = slice((n % FC) * P, (n % FC + 1) * P)
                            if before or n >= 4:
                                pe.wait_ge(h_gated, c * HN + (n - 3))
                            if n == LAGH and (not isinstance(c, int) or c >= 2):
                                pe.wait_ge(y_copied, c - 1)
                            o = h_ps[:, n % 4, :]
                            nc.tensor.matmul(o, w1h[:, e, part], xh[:, cols], start=True, stop=False)
                            nc.tensor.matmul(o, w1h[:, e, part], xl[:, cols], start=False, stop=False)
                            nc.tensor.matmul(o, w1l[:, e, part], xh[:, cols], start=False,
                                             stop=True).then_inc(h_done, 1)
                        if n >= LAGH and now or n < LAGH and before:
                            m = (n - LAGH) % HN
                            slot = s if n >= LAGH else 1 - s
                            o = y_ps[:, slot, :]
                            if m == 0:
                                nc.tensor.matmul(o, b2_sb[:], gT[:, cols], start=True, stop=False)
                            pe.wait_ge(h_low_done, c * HN + (n - LAGH + 1))
                            w2_high, w2_low = [w[:, m // FC, m % FC, :] for w in (w2h, w2l)]
                            nc.tensor.matmul(o, w2_high, h_high[:, m % 4, :], start=False, stop=False)
                            nc.tensor.matmul(o, w2_low, h_high[:, m % 4, :], start=False, stop=False)
                            nc.tensor.matmul(o, w2_high, h_low[:, m % 4, :], start=False,
                                             stop=m == HN - 1).then_inc(h_used, 1)
                        if n == TURN_AT and before:
                            pe.wait_ge(y_copied, c)
                            if not isinstance(c, int) or c > 1:
                                pe.wait_ge(y_read, c - 1)
                            for t in range(CT):
                                last = nc.tensor.transpose(yt_ps[:, t, :], y_sb[:, t * P:(t + 1) * P], ident[:])
                            last.then_inc(y_turned, 1)

                each_chunk(pe, chunk)

            @block.scalar
            def _(act):
                def chunk(pair, s, before, now):
                    c = pair * 2 + s
                    for n in range(HN):
                        if now:
                            act.wait_ge(h_gated, c * HN + (n + 1))
                            if before or n >= 4:
                                act.wait_ge(h_used, c * HN + (n - 3))
                            nc.scalar.activation(h_high[:, n % 4, :], h_sb[:, n % 4, :], ACT.Relu)
                            if before or n >= 2:
                                act.wait_ge(h_low_done, c * HN + (n - 1))
                            nc.scalar.activation(h_full[:, n % 2, :], h_sb[:, n % 4, :], ACT.Relu).then_inc(
                                h_relu_done, 1)
                        if n == COPY_AT and before:
                            act.wait_ge(h_used, c * HN)
                            if not isinstance(c, int) or c > 1:
                                act.wait_ge(y_turned, c - 1)
                            nc.scalar.copy(y_sb[:], y_ps[:, 1 - s, :]).then_inc(y_copied, 1)
                        if n == ROOT_AT and before:
                            act.wait_ge(var4, c)
                            nc.scalar.activation(root_sb[:], var_sb[:], ACT.Sqrt).then_inc(root4, 1)

                each_chunk(act, chunk)

            @block.vector
            def _(dve):
                def residual(c):
                    dve.wait_ge(y_turned, c)
                    nc.vector.tensor_tensor(z_sb[:], yt_ps[:], x_sb[:, bass.ds((c - 1) * CT, CT), :],
                                            ALU.add).then_inc(y_read, 1)
                    dve.wait_ge(y_read, c)
                    for t in range(CT):
                        last = nc.vector.bn_stats(stats4[:, t, :], z_sb[:, t, :])
                    last.then_inc(chain4, 1)

                def variance(c):
                    link = (c - 1) * LINKS
                    dve.wait_ge(chain4, link + 1)
                    nc.vector.memset(pause[:], 0.0)
                    for t in range(CT):
                        last = nc.vector.bn_aggr(mv4[:, t, :], stats4[:, t, :])
                    last.then_inc(chain4, 1)
                    dve.wait_ge(chain4, link + 2)
                    nc.vector.tensor_scalar(var_sb[:], mv4[:, :, 1], EPS, None, ALU.add).then_inc(var4, 1)

                def scale(pair, c, s, tiles):
                    link = (c - 1) * LINKS
                    if tiles[0] == 0:
                        dve.wait_ge(root4, c)
                        nc.vector.reciprocal(rstd_sb[:], root_sb[:]).then_inc(chain4, 1)
                        dve.wait_ge(chain4, link + 3)
                        if not isinstance(c, int) or c > 2:
                            dve.wait_ge(out_stored[0], pair * 16)
                    for t in tiles:
                        last = nc.vector.tensor_scalar(out_sb[:, 1 - s, t, :], z_sb[:, t, :], mv4[:, t, 0:1],
                                                       rstd_sb[:, t:t + 1], ALU.subtract, ALU.mult)
                    if tiles[-1] == CT - 1:
                        last.then_inc(out_ready, 1)

                def chunk(pair, s, before, now):
                    c = pair * 2 + s
                    for n in range(HN):
                        if now:
                            dve.wait_ge(h_done, c * HN + (n + 1))
                            if n % (HE * FC) == 0:
                                dve.wait_ge(gates_spread[n // (HE * FC)], c * 16 + 16)
                            if before or n >= 4:
                                dve.wait_ge(h_relu_done, c * HN + (n - 3))
                            nc.vector.scalar_tensor_tensor(h_sb[:, n % 4, :], h_ps[:, n % 4, :], b1_sb[:, n:n + 1],
                                                           gate_sb[:, n // (HE * FC), (n // FC) % HE, :], ALU.add,
                                                           ALU.mult).then_inc(h_gated, 1)
                        if n == NORM_AT and before:
                            residual(c)
                        if n == VAR_AT and before:
                            variance(c)
                        if n in SCALE_AT and before:
                            first = SCALE_AT.index(n) * (CT // 2)
                            scale(pair, c, s, range(first, first + CT // 2))

                each_chunk(dve, chunk)

            @block.gpsimd
            def _(pool):
                def chunk(pair, s, before, now):
                    c = pair * 2 + s
                    if not now:
                        return
                    for n in range(HN):
                        pool.wait_ge(h_relu_done, c * HN + (n + 1))
                        if before or n >= 4:
                            pool.wait_ge(h_used, c * HN + (n - 3))
                        nc.gpsimd.tensor_tensor(h_low[:, n % 4, :], h_full[:, n % 2, :],
                                                h_high[:, n % 4, :].bitcast(F32), ALU.subtract).then_inc(h_low_done, 1)

                each_chunk(pool, chunk)

            @block.sync
            def _(sp):
                def next_gates(c, half):
                    sp.wait_ge(h_gated, (c - 1) * HN + (half + 1) * HE * FC)
                    spread_gates(sp, c, half)

                sp.wait_ge(g_stored, 16)
                for c in range(CHUNKS + 1):
                    if c < CHUNKS - 1:
                        next_gates(c + 1, 0)
                    if c:
                        if c > 1:
                            sp.wait_ge(out_stored[c % 2], 16 * (c // 2))
                        sp.wait_ge(out_ready, c)
                        sp.dma_start(out[(c - 1) * CT:c * CT].rearrange("t p d -> p t d"),
                                     out_sb[:, (c - 1) % 2]).then_inc(out_stored[(c - 1) % 2], 16)
                    if c < CHUNKS - 1:
                        next_gates(c + 1, 1)
                for s in range(2):
                    sp.wait_ge(out_stored[s], 16 * (CHUNKS // 2))

        ffn.close()


def sinusoids():
    inv = np.float32(1.0) / np.float32(10000.0) ** (np.arange(0, D, 2, dtype=np.float32) / np.float32(D))
    ang = np.arange(-(L - 1), L, dtype=np.float32)[:, None] * inv[None, :].astype(np.float32)
    emb = np.zeros((2 * L - 1, D), np.float32)
    emb[:, 0::2] = np.sin(ang)
    emb[:, 1::2] = np.cos(ang)
    low = np.zeros((D, REL_PAD), np.float32)
    up = np.zeros((D, REL_PAD), np.float32)
    low[:, 0:L] = emb.T[:, L - 1:2 * L - 1]
    up[:, L + 1:2 * L - 1] = emb.T[:, 0:L - 2]
    return low, up


def kernel(L0_attn_w, L0_attn_Wq, L0_attn_Wk, L0_attn_Wv, L0_attn_Wr, L0_attn_u_bias, L0_attn_v_bias, L0_ffn_Wg,
           L0_ffn_bg, L0_ffn_W1, L0_ffn_b1, L0_ffn_W2, L0_ffn_b2):
    import concourse.bacc as bacc
    from concourse.bass_utils import run_bass_kernel_spmd

    w = np.asarray(L0_attn_w)
    low, up = sinusoids()
    arrays = {
        "w_tok": w.reshape(B, NHI, HALF, LO, D).transpose(0, 2, 1, 3, 4).reshape(TILES, P, D),
        "wT": w.reshape(TOK, D).T,
        "WqT": np.asarray(L0_attn_Wq).T,
        "WkT": np.asarray(L0_attn_Wk).T,
        "WvT": np.asarray(L0_attn_Wv).T,
        "WrT": np.asarray(L0_attn_Wr).T,
        "u_bias": np.asarray(L0_attn_u_bias).reshape(D, 1),
        "v_bias": np.asarray(L0_attn_v_bias).reshape(D, 1),
        "sin_low": low,
        "sin_up": up,
        "ident_in": np.eye(P, dtype=np.float32),
        "order_in": np.tile(np.arange(E, 2 * E, dtype=np.float32), (P, 1)),
        "Wg": np.asarray(L0_ffn_Wg),
        "bg": np.asarray(L0_ffn_bg),
        "W1": np.asarray(L0_ffn_W1),
        "b1T": np.asarray(L0_ffn_b1).reshape(HN, P).T,
        "W2": np.asarray(L0_ffn_W2),
        "b2": np.asarray(L0_ffn_b2),
    }
    arrays = {f"{n}_dram": np.ascontiguousarray(a) for n, a in arrays.items()}
    nc = bacc.Bacc("TRN2", target_bir_lowering=False, num_devices=1)
    args = [nc.dram_tensor(n, a.shape, F32, kind="ExternalInput").ap() for n, a in arrays.items()]
    out = nc.dram_tensor("out_dram", (TILES, P, D), F32, kind="ExternalOutput").ap()
    attention_moe_kernel(nc, *args, out)
    r = run_bass_kernel_spmd(nc, [arrays], core_ids=[0])
    y = r.results[0]["out_dram"]
    return y.reshape(B, HALF, NHI, LO, D).transpose(0, 2, 1, 3, 4).reshape(B, L, D)
```

```python
from contextlib import ExitStack

import numpy as np

import concourse.bass as bass
from concourse import mybir

F32 = mybir.dt.float32
F32R = mybir.dt.float32r
ALU = mybir.AluOpType
ACT = mybir.ActivationFunctionType
AX = mybir.AxisListType

P = 128
B, L, D = 16, 256, 128
H = 16
DH = D // H
E, F = 8, 512
FC = F // P
TOK = B * L
SCALE = 1.0 / float(np.sqrt(np.float32(DH)))
EPS = 1e-5

NHI = 8
HALF = 2
LO = 16
SHIFT = HALF * LO
NREL = L + SHIFT
REL_PAD = 2 * L
GB = 2
GS = 2 * GB
NG = B // GB
STEP_TILES = 4
UNIT_STEPS = LO // STEP_TILES
PAIR = 2
PAIRS = H // PAIR
PAIR_UNITS = PAIR * HALF
PAIR_STEPS = PAIR_UNITS * UNIT_STEPS
STEPS = PAIRS * PAIR_STEPS
VG = 4
VE = DH + 1
VW = 32
PV_LAG = UNIT_STEPS + 1
OUT_LAG = PV_LAG + UNIT_STEPS
TAIL = PV_LAG + 1
EARLY = B - 2 * GB
TILES = TOK // P
CHUNK = 512
CHUNKS = TOK // CHUNK
CT = CHUNK // P
HN = E * FC


def attention_moe_kernel(nc, w_tok, wT, WqT, WkT, WvT, WrT, u_bias, v_bias, sin_low, sin_up, ident_in, order_in,
                         Wg, bg, W1, b1T, W2, b2, out):
    with ExitStack() as whole:
        def sem(name):
            return whole.enter_context(nc.semaphore(name))

        def alloc(stack, name, shape, dt=F32):
            return stack.enter_context(nc.sbuf_tensor(name, shape, dt))

        def psum(stack, name, shape):
            return stack.enter_context(nc.psum_tensor(name, shape, F32))

        q_rel_dram = nc.dram_tensor("q_rel_dram", [D, HALF, NHI, 2, B, 2, LO], F32).ap()
        q_key_dram = nc.dram_tensor("q_key_dram", [D, HALF, B, NHI, 2, LO], F32).ap()
        key_dram = nc.dram_tensor("key_dram", [D, B, L], F32).ap()
        rel_table = nc.dram_tensor("rel_dram", [D, 2, REL_PAD], F32)
        rel_dram = rel_table.ap()
        rel_windows = bass.AP(rel_table, 0, [[DH * 2 * REL_PAD, H], [SHIFT, NHI], [REL_PAD, DH * 2], [1, NREL]])

        gate_dram = nc.dram_tensor("gate_dram", [E, TOK], F32).ap()

        attn = alloc(whole, "attn", [P, TILES, D])
        x_sb = alloc(whole, "x_sb", [P, TILES, D])
        ident = alloc(whole, "ident", [P, P])

        att = ExitStack()
        v_all = alloc(att, "v_all", [P, TILES, H, DH + 1])
        q_rel = alloc(att, "q_rel", [P, HALF, NHI, B, 2, LO], F32R)
        q_key = alloc(att, "q_key", [P, HALF, NHI, B, 2, LO], F32R)
        keys = alloc(att, "keys", [P, PAIR, 2, L], F32R)
        rel = alloc(att, "rel", [P, PAIR, 2, NREL], F32R)
        head_full = alloc(att, "head_full", [P, L + NREL])

        def load_content(eng, rows, half, batches, loaded):
            for b in batches:
                eng.dma_start(
                    q_key[b * DH:(b + 1) * DH, half, :, b].bitcast(F32).rearrange("p h t x -> p h (t x)"),
                    q_key_dram[rows, half, b].rearrange("d h t x -> d h (t x)")).then_inc(loaded, 16)

        bias_loaded = sem("bias_loaded")
        wq_loaded = sem("wq_loaded")
        wkv_loaded = sem("wkv_loaded")
        wr_loaded = sem("wr_loaded")
        ident_loaded = sem("ident_loaded")
        wt_loaded = [sem(f"wt_loaded{i}") for i in range(4)]
        biases_scaled = sem("biases_scaled")
        rel_done = sem("rel_done")
        rel_copied = sem("rel_copied")
        q_done = sem("q_done")
        k_done = sem("k_done")
        v_done = sem("v_done")
        u_full = sem("u_full")
        q_full = sem("q_full")
        k_full = sem("k_full")
        v_copied = sem("v_copied")
        content_high = sem("content_high")
        content_low = sem("content_low")
        high_done = sem("high_done")
        low_done = sem("low_done")
        stored = [sem(f"stored{i}") for i in range(2)]
        q_stored = [sem(f"q_stored{i}") for i in range(2)]
        rel_stored = sem("rel_stored")
        head_loaded = sem("head_loaded")
        head_high = sem("head_high")
        head_split = sem("head_split")
        q_loaded = [sem(f"q_loaded{i}") for i in range(HALF)]
        zeroed = sem("zeroed")
        first_content = sem("first_content")
        first_rel_loaded = sem("first_rel_loaded")
        STORES = 2

        with ExitStack() as st:
            wT_sb = attn[:].rearrange("p t d -> p (t d)")
            wq_sb = alloc(st, "wq_sb", [P, D])
            wk_sb = alloc(st, "wk_sb", [P, D])
            wv_sb = alloc(st, "wv_sb", [P, D])
            wr_sb = alloc(st, "wr_sb", [P, D])
            sins = alloc(st, "sins", [P, 2, REL_PAD])
            bias = alloc(st, "bias", [P, 4])
            rel_sb = alloc(st, "rel_sb", [P, 2, REL_PAD])
            full_v = alloc(st, "full_v", [P, 2, GB, L + SHIFT])
            full_u = alloc(st, "full_u", [P, 2, GB, L])
            full_k = alloc(st, "full_k", [P, 2, GB, L])
            stage_rel = alloc(st, "stage_rel", [P, 2, HALF, NHI, 2, GS, 2, LO], F32R)
            stage_q = alloc(st, "stage_q", [P, 2, HALF, GB, NHI, 2, LO], F32R)
            rel_ps = psum(st, "rel_ps", [P, 2, REL_PAD])
            q_ps = psum(st, "q_ps", [P, 2, CHUNK])
            k_ps = psum(st, "k_ps", [P, 2, CHUNK])
            v_ps = psum(st, "v_ps", [P, 2, CT, D])
            block = st.enter_context(nc.Block())

            def rel_view(slot, up, half):
                start = half * LO + up
                return full_v[:, slot, :, start:start + L].rearrange("p b (h x) -> p h b x", x=SHIFT)[:, :, :, 0:LO]

            def stage_view(c, up, half, part):
                place = (c % 2) * GB
                return stage_rel[:, (c // 2) % 2, half, :, up, place:place + GB, part, :]

            def key_view(slot, half):
                return full_u[:, slot].rearrange("p b (h a l) -> p b h a l", h=NHI, a=HALF)[:, :, :, half, :]

            @block.sync
            def _(sp):
                def load_tokens(c):
                    part = slice(c * 1024, (c + 1) * 1024)
                    sp.dma_start(wT_sb[:, part], wT[:, part]).then_inc(wt_loaded[c], 16)

                sp.dma_start(wq_sb[:], WqT).then_inc(wq_loaded, 16)
                load_tokens(0)
                sp.dma_start(bias[:, 0:1], u_bias).then_inc(bias_loaded, 16)
                sp.dma_start(bias[:, 1:2], v_bias).then_inc(bias_loaded, 16)
                sp.dma_start(wk_sb[:], WkT).then_inc(wkv_loaded, 16)
                sp.dma_start(wv_sb[:], WvT).then_inc(wkv_loaded, 16)
                load_tokens(1)
                sp.dma_start(wr_sb[:], WrT).then_inc(wr_loaded, 16)
                sp.dma_start(sins[:, 0, :], sin_low).then_inc(wr_loaded, 16)
                sp.dma_start(sins[:, 1, :], sin_up).then_inc(wr_loaded, 16)
                load_tokens(2)
                load_tokens(3)
                sp.dma_start(ident[:], ident_in).then_inc(ident_loaded, 16)
                for c in range(NG):
                    slot = c % 2
                    sp.wait_ge(k_full, c + 1)
                    sp.wait_ge(content_high, c + 1)
                    sp.wait_ge(content_low, c + 1)
                    sp.dma_start(
                        q_key_dram[:, :, c * GB:(c + 1) * GB].rearrange("p a b h t x -> p a (b h t x)"),
                        stage_q[:, slot].bitcast(F32).rearrange("p a b h t x -> p a (b h t x)")).then_inc(
                            stored[slot], 16)
                    sp.dma_start(
                        key_dram[:, c * GB:(c + 1) * GB, :].rearrange("p b x -> p (b x)"),
                        full_k[:, slot].rearrange("p b x -> p (b x)")).then_inc(stored[slot], 16)
                    if c == 1:
                        sp.wait_ge(rel_copied, 1)
                        sp.dma_start(rel_dram, rel_sb[:]).then_inc(rel_stored, 16)
                    if c % 2 == 1:
                        sp.wait_ge(high_done, c + 1)
                        sp.wait_ge(low_done, c + 1)
                        first = (c - 1) * GB
                        sp.dma_start(
                            q_rel_dram[:, :, :, :, first:first + GS].rearrange("p a h u b t x -> p (a h u) (b t x)"),
                            stage_rel[:, (c // 2) % 2].bitcast(F32).rearrange(
                                "p a h u b t x -> p (a h u) (b t x)")).then_inc(q_stored[(c // 2) % 2], 16)
                sp.wait_ge(rel_stored, 16)
                sp.dma_start(head_full[:, L:L + NREL], rel_windows[0]).then_inc(first_rel_loaded, 16)
                for slot in range(2):
                    sp.wait_ge(stored[slot], 16 * STORES * (NG // 2))
                    sp.wait_ge(q_stored[slot], 16 * (NG // 4))
                sp.wait_ge(ident_loaded, 16)

            @block.tensor
            def _(pe):
                pe.wait_ge(wq_loaded, 16)
                for c in range(NG):
                    slot = c % 2
                    if c % 2 == 0:
                        pe.wait_ge(wt_loaded[c // 2], 16)
                    cols = wT_sb[:, c * CHUNK:(c + 1) * CHUNK]
                    if c >= 2:
                        pe.wait_ge(q_full, c - 1)
                    nc.tensor.matmul(q_ps[:, slot, :], wq_sb[:], cols, start=True, stop=True).then_inc(q_done, 1)
                    if c == 0:
                        pe.wait_ge(wkv_loaded, 16 * 2)
                    if c >= 2:
                        pe.wait_ge(k_full, c - 1)
                    nc.tensor.matmul(k_ps[:, slot, :], wk_sb[:], cols, start=True, stop=True).then_inc(k_done, 1)
                    if c >= 2:
                        pe.wait_ge(v_copied, c - 1)
                    for t in range(CT):
                        last = nc.tensor.matmul(v_ps[:, slot, t, :], cols[:, t * P:(t + 1) * P], wv_sb[:],
                                                start=True, stop=True)
                    last.then_inc(v_done, 1)
                    if c == 1:
                        pe.wait_ge(wr_loaded, 16 * 3)
                        for up in range(2):
                            last = nc.tensor.matmul(rel_ps[:, up, :], wr_sb[:], sins[:, up, :], start=True, stop=True)
                        last.then_inc(rel_done, 1)

            @block.scalar
            def _(act):
                act.wait_ge(biases_scaled, 1)
                for c in range(NG):
                    slot = c % 2
                    if c >= 2:
                        act.wait_ge(low_done, c - 1)
                        act.wait_ge(stored[slot], 16 * STORES * (c // 2))
                    if c >= 4:
                        act.wait_ge(q_stored[(c // 2) % 2], 16 * (c // 4))
                    act.wait_ge(q_done, c + 1)
                    src = q_ps[:, slot, :].rearrange("p (b i) -> p b i", b=GB)
                    nc.scalar.activation(full_u[:, slot], src, ACT.Identity, bias=bias[:, 2:3],
                                         scale=SCALE).then_inc(u_full, 1)
                    nc.scalar.activation(full_v[:, slot, :, 0:L], src, ACT.Identity,
                                         bias=bias[:, 3:4], scale=SCALE).then_inc(q_full, 1)
                    act.wait_ge(k_done, c + 1)
                    nc.scalar.copy(full_k[:, slot], k_ps[:, slot, :].rearrange("p (b i) -> p b i", b=GB)).then_inc(
                        k_full, 1)
                    act.wait_ge(u_full, c + 1)
                    for half in range(HALF):
                        last = nc.scalar.copy(stage_q[:, slot, half, :, :, 0, :], key_view(slot, half))
                    last.then_inc(content_high, 1)
                    act.wait_ge(q_full, c + 1)
                    for up in range(2):
                        for half in range(HALF):
                            last = nc.scalar.copy(stage_view(c, up, half, 0), rel_view(slot, up, half))
                    last.then_inc(high_done, 1)
                    if c == 1:
                        act.wait_ge(rel_done, 1)
                        nc.scalar.copy(rel_sb[:], rel_ps[:]).then_inc(rel_copied, 1)

            @block.vector
            def _(dve):
                nc.vector.memset(full_v[:, :, :, L:L + SHIFT], 0.0)
                nc.vector.memset(v_all[:, :, :, DH:DH + 1], 1.0)
                dve.wait_ge(bias_loaded, 16 * 2)
                nc.vector.tensor_scalar(bias[:, 2:4], bias[:, 0:2], SCALE, None, ALU.mult).then_inc(biases_scaled, 1)
                for c in range(NG):
                    slot = c % 2
                    dve.wait_ge(v_done, c + 1)
                    nc.vector.tensor_copy(v_all[:, CT * c:CT * (c + 1), :, 0:DH],
                                          v_ps[:, slot].rearrange("p t (h d) -> p t h d", h=H)).then_inc(v_copied, 1)
                    dve.wait_ge(content_high, c + 1)
                    for half in range(HALF):
                        low, high = [stage_q[:, slot, half, :, :, part, :] for part in (1, 0)]
                        last = nc.vector.tensor_tensor(low, key_view(slot, half), high.bitcast(F32), ALU.subtract)
                    last.then_inc(content_low, 1)
                    dve.wait_ge(high_done, c + 1)
                    for up in range(2):
                        for half in range(HALF):
                            low, high = [stage_view(c, up, half, part) for part in (1, 0)]
                            last = nc.vector.tensor_tensor(low, rel_view(slot, up, half), high.bitcast(F32),
                                                           ALU.subtract)
                    last.then_inc(low_done, 1)

            @block.gpsimd
            def _(pool):
                nc.gpsimd.memset(q_rel[:].bitcast(F32), 0.0)
                nc.gpsimd.memset(q_key[:].bitcast(F32), 0.0).then_inc(zeroed, 1)
                pool.wait_ge(zeroed, 1)
                pool.wait_ge(content_high, NG)
                load_content(pool, slice(0, DH), 0, range(EARLY), first_content)

        x_loaded = sem("x_loaded")
        scores_done = sem("scores_done")
        max_done = sem("max_done")
        exp_done = sem("exp_done")
        turned = sem("turned")
        pv_done = sem("pv_done")
        o_copied = sem("o_copied")
        o_turned = sem("o_turned")
        recip_done = sem("recip_done")
        v_padded = sem("v_padded")
        v_high = sem("v_high")
        v_ready = sem("v_ready")
        turned_high = sem("turned_high")
        turned_low = sem("turned_low")
        low_moved = sem("low_moved")
        summed = sem("summed")
        Q_LOADED = 16 * (NHI + B)
        HEAD_LOADED = 16 * 2

        with ExitStack() as st:
            probsT = alloc(st, "probsT", [P, 2, 2, 2, NHI, B, LO], F32R)
            probs = alloc(st, "probs", [P, 2, STEP_TILES, L])
            v_head = alloc(st, "v_head", [P, PAIR, TILES, VW], F32R)
            v_full = alloc(st, "v_full", [P, TILES, DH])
            o_sb = alloc(st, "o_sb", [VG * VW, P])
            neg_max = alloc(st, "neg_max", [P, 2, STEP_TILES])
            low_sums = alloc(st, "low_sums", [P, B, VE])
            sums = alloc(st, "sums", [P, B, VE])
            recip = alloc(st, "recip", [P, B])
            s_ps = psum(st, "s_ps", [P, 2, STEP_TILES, L])
            t_ps = psum(st, "t_ps", [P, 2, 2, 2, P])
            o_ps = psum(st, "o_ps", [VW, VG, P])
            ot_ps = psum(st, "ot_ps", [P, B, VW])
            o_last = s_ps[0:VW, 0, 0:2, :].rearrange("p t (h x) -> p (t h) x", x=P)
            block = st.enter_context(nc.Block())

            def o_bank(at):
                return o_last if at > STEPS and (at - STEPS) % 2 == 1 else o_ps

            def each_step(eng, step):
                for k in range(PAIR_STEPS):
                    step(0, k, k)
                with eng.Fori(1, PAIRS) as pair:
                    for k in range(PAIR_STEPS):
                        step(pair, k, PAIR_STEPS + k)
                for k in range(TAIL):
                    step(PAIRS, k, STEPS + k)

            def turned_views(unit, v, c):
                lo = (v % UNIT_STEPS) * STEP_TILES + 2 * c
                return [probsT[:, unit % 2, part, :, :, :, lo:lo + 2].rearrange("p j h b t -> p t j (h b)")
                        for part in range(2)]

            @block.sync
            def _(sp):
                def load_pair(pair, first):
                    for k in range(PAIR_UNITS):
                        hd = k // HALF
                        half = k % HALF
                        rows = bass.ds(pair * (PAIR * DH) + hd * DH, DH)
                        if not (first and k < 2):
                            sp.wait_ge(scores_done, pair * PAIR_STEPS + (k - 1) * UNIT_STEPS)
                        if half == 0:
                            sp.dma_start(head_full[:, 0:L],
                                         key_dram[rows].rearrange("d b x -> b d x")).then_inc(head_loaded, 16)
                            if not (first and k == 0):
                                sp.dma_start(head_full[:, L:L + NREL],
                                             rel_windows[bass.ds(pair * PAIR + hd, 1)].rearrange(
                                                 "o g r x -> (o g) r x")).then_inc(head_loaded, 16)
                        for hi in range(NHI):
                            r = (NHI - 1 - hi) * 2 * DH
                            sp.dma_start(
                                q_rel[r:r + 2 * DH, half, hi].bitcast(F32).rearrange("p b t x -> p (b t x)"),
                                q_rel_dram[rows, half, hi].rearrange("d u b t x -> d u (b t x)")).then_inc(
                                    q_loaded[half], 16)
                        if not (first and k == 0):
                            load_content(sp, rows, half, range(B), q_loaded[half])

                load_pair(0, True)
                sp.dma_start(x_sb[:], w_tok.rearrange("t p d -> p t d")).then_inc(x_loaded, 16)
                with sp.Fori(1, PAIRS) as pair:
                    load_pair(pair, False)

            @block.gpsimd
            def _(pool):
                load_content(pool, slice(0, DH), 0, range(EARLY, B), first_content)
                nc.gpsimd.memset(v_head[:].bitcast(F32), 0.0).then_inc(v_padded, 1)
                pool.wait_ge(v_padded, 1)

                def split_head(pair, hd, first):
                    pool.wait_ge(head_loaded, pair * (PAIR * HEAD_LOADED) + ((hd + 1) * HEAD_LOADED - 16))
                    if first and hd == 0:
                        pool.wait_ge(first_rel_loaded, 16)
                    one = v_all[:, 0, 0, DH:DH + 1]
                    for part, cols in ((keys, head_full[:, 0:L]), (rel, head_full[:, L:L + NREL])):
                        last = nc.gpsimd.tensor_tensor(part[:, hd, 0, :], cols,
                                                       one.to_broadcast([P, cols.shape[1]]), ALU.mult)
                    last.then_inc(head_high, 1)
                    pool.wait_ge(head_high, pair * PAIR + (hd + 1))
                    nc.gpsimd.tensor_tensor(keys[:, hd, 1, :], head_full[:, 0:L], keys[:, hd, 0, :].bitcast(F32),
                                            ALU.subtract)
                    nc.gpsimd.tensor_tensor(rel[:, hd, 1, :], head_full[:, L:L + NREL],
                                            rel[:, hd, 0, :].bitcast(F32), ALU.subtract).then_inc(head_split, 1)

                def values(pair, first):
                    for hd in range(PAIR):
                        split_head(pair, hd, first)
                        if not first:
                            pool.wait_ge(pv_done, pair * PAIR_STEPS + (hd - 1) * HALF * UNIT_STEPS)
                        if not (first and hd == 0):
                            pool.wait_ge(v_ready, pair * PAIR + hd)
                        full = v_all[:, :, bass.ds(pair * PAIR + hd, 1), :].rearrange("p t h d -> p t (h d)")
                        nc.gpsimd.tensor_copy(v_head[:, hd, :, 0:VE], full)
                        nc.gpsimd.tensor_copy(v_full[:], full[:, :, 0:DH]).then_inc(v_high, 1)
                        pool.wait_ge(v_high, pair * PAIR + (hd + 1))
                        nc.gpsimd.tensor_tensor(v_head[:, hd, :, VE:VE + DH], v_full[:],
                                                v_head[:, hd, :, 0:DH].bitcast(F32),
                                                ALU.subtract).then_inc(v_ready, 1)

                values(0, True)
                with pool.Fori(1, PAIRS) as pair:
                    values(pair, False)

            @block.tensor
            def _(pe):
                def scores(pair, k, at):
                    unit = k // UNIT_STEPS
                    half = unit % HALF
                    hd = unit // HALF
                    if k % UNIT_STEPS == 0:
                        other_queue = 16 * B if half == 0 else 0
                        pe.wait_ge(q_loaded[half],
                                   pair * (PAIR * Q_LOADED) + ((unit // HALF + 1) * Q_LOADED - other_queue))
                        if at == 0:
                            pe.wait_ge(first_content, 16 * B)
                        if half == 0:
                            pe.wait_ge(head_split, pair * PAIR + (hd + 1))
                    if at >= 2:
                        pe.wait_ge(exp_done, pair * PAIR_STEPS + (k - 1))
                    for t in range(STEP_TILES):
                        lo = (k % UNIT_STEPS) * STEP_TILES + t
                        start = SHIFT - 1 - (half * LO + lo)
                        q_r = [q_rel[:, half, :, :, x, lo].rearrange("p h b -> p (h b)") for x in range(2)]
                        r = [rel[:, hd, x, start:start + L] for x in range(2)]
                        q_k = [q_key[:, half, :, :, x, lo].rearrange("p h b -> p (h b)") for x in range(2)]
                        ks = [keys[:, hd, x, :] for x in range(2)]
                        o = s_ps[:, k % 2, t, :]
                        nc.tensor.matmul(o, q_r[0], r[0], start=True, stop=False)
                        nc.tensor.matmul(o, q_r[0], r[1], start=False, stop=False)
                        nc.tensor.matmul(o, q_r[1], r[0], start=False, stop=False)
                        nc.tensor.matmul(o, q_k[0], ks[0], start=False, stop=False)
                        nc.tensor.matmul(o, q_k[0], ks[1], start=False, stop=False)
                        last = nc.tensor.matmul(o, q_k[1], ks[0], start=False, stop=True)
                    last.then_inc(scores_done, 1)

                def turn_out(pair, k, at):
                    v = k - PV_LAG - 1
                    q = v % UNIT_STEPS
                    pe.wait_ge(o_copied, pair * PAIR_STEPS + (v + 1))
                    if q == 0 and at > PV_LAG + UNIT_STEPS:
                        pe.wait_ge(summed, pair * PAIR_UNITS + v // UNIT_STEPS)

                    nc.tensor.transpose(ot_ps[:, q * VG:(q + 1) * VG, :].rearrange("p g x -> p (g x)"), o_sb[:],
                                        ident[:]).then_inc(o_turned, 1)

                def values(pair, k, at):
                    v = k - PV_LAG
                    q = v % UNIT_STEPS
                    unit = v // UNIT_STEPS
                    hd = (unit // HALF) % PAIR
                    if q == 0:
                        pe.wait_ge(turned_low, pair * (2 * PAIR_STEPS) + 2 * (v + UNIT_STEPS))
                        pe.wait_ge(v_ready, pair * PAIR + (unit // HALF + 1))
                    if PV_LAG < at <= STEPS:
                        pe.wait_ge(o_copied, pair * PAIR_STEPS + v)
                    elif at > STEPS + 1:
                        pe.wait_ge(o_copied, pair * PAIR_STEPS + (v - 1))
                    for g in range(VG):
                        b = q * VG + g
                        for n in range(4):
                            part, jh = n // 2, n % 2
                            last = nc.tensor.matmul(o_bank(at)[:, g, :], v_head[:, hd, 2 * b + jh, :],
                                                    probsT[:, unit % 2, part, jh, :, b, :], start=n == 0, stop=n == 3)
                    last.then_inc(pv_done, 1)

                def turn_probs(pair, k, at):
                    pe.wait_ge(exp_done, pair * PAIR_STEPS + k)
                    for c in range(2):
                        if at >= 2:
                            pe.wait_ge(turned_low, pair * (2 * PAIR_STEPS) + (2 * (k - 1) + c - 1))
                        for t in range(2):
                            for jh in range(2):
                                last = nc.tensor.transpose(t_ps[:, c, t, jh, :],
                                                           probs[:, (k - 1) % 2, 2 * c + t, jh * P:(jh + 1) * P],
                                                           ident[:])
                        last.then_inc(turned, 1)

                def step(pair, k, at):
                    if at < STEPS:
                        scores(pair, k, at)
                    if 1 <= at <= STEPS:
                        turn_probs(pair, k, at)
                    if PV_LAG < at <= STEPS:
                        turn_out(pair, k, at)
                    if PV_LAG <= at < STEPS + PV_LAG:
                        values(pair, k, at)
                    if STEPS < at:
                        turn_out(pair, k, at)

                each_step(pe, step)

            @block.vector
            def _(dve):
                def low_parts(pair, k, c):
                    v = k - 1
                    dve.wait_ge(turned_high, pair * (2 * PAIR_STEPS) + (2 * v + c + 1))
                    high, low = turned_views(v // UNIT_STEPS, v, c)
                    nc.vector.tensor_tensor(low, t_ps[:, c], high.bitcast(F32), ALU.subtract).then_inc(turned_low, 1)

                def step(pair, k, at):
                    if at < STEPS:
                        dve.wait_ge(scores_done, pair * PAIR_STEPS + (k + 1))
                        nc.vector.tensor_reduce(neg_max[:, k % 2, :], s_ps[:, k % 2], axis=AX.X, op=ALU.max,
                                                negate=True).then_inc(max_done, 1)
                    if 1 <= at <= STEPS:
                        for c in range(2):
                            low_parts(pair, k, c)
                    if PV_LAG <= at < STEPS + PV_LAG:
                        v = k - PV_LAG
                        dve.wait_ge(pv_done, pair * PAIR_STEPS + (v + 1))
                        if at > PV_LAG:
                            dve.wait_ge(o_turned, pair * PAIR_STEPS + v)
                        for g in range(VG):
                            last = nc.vector.tensor_copy(o_sb[g * VW:(g + 1) * VW, :], o_bank(at)[:, g, :])
                        last.then_inc(o_copied, 1)
                    out = at >= OUT_LAG and (k - OUT_LAG) % UNIT_STEPS == 0
                    n = (k - OUT_LAG) // UNIT_STEPS
                    if out:
                        dve.wait_ge(o_turned, pair * PAIR_STEPS + (n + 1) * UNIT_STEPS)
                        nc.vector.tensor_copy(low_sums[:], ot_ps[:, :, VE:2 * VE]).then_inc(low_moved, 1)
                        dve.wait_ge(low_moved, pair * PAIR_UNITS + (n + 1))
                        nc.vector.tensor_tensor(sums[:], ot_ps[:, :, 0:VE], low_sums[:], ALU.add).then_inc(summed, 1)
                        dve.wait_ge(summed, pair * PAIR_UNITS + (n + 1))
                        nc.vector.reciprocal(recip[:], sums[:, :, DH]).then_inc(recip_done, 1)
                        dve.wait_ge(recip_done, pair * PAIR_UNITS + (n + 1))
                        head_cols = bass.ds(pair * (PAIR * DH) + (n // HALF) * DH, DH)
                        dst = attn[:].rearrange("p (b a) d -> p b a d", a=HALF)[:, :, n % HALF, head_cols]
                        nc.vector.tensor_tensor(dst, sums[:, :, 0:DH], recip[:].unsqueeze(2).to_broadcast([P, B, DH]),
                                                ALU.mult)

                each_step(dve, step)

            @block.scalar
            def _(act):
                def step(pair, k, at):
                    if 1 <= at <= STEPS:
                        v = k - 1
                        unit = v // UNIT_STEPS
                        for c in range(2):
                            if v % UNIT_STEPS == 0 and c == 0 and at > 2 * UNIT_STEPS:
                                act.wait_ge(pv_done, pair * PAIR_STEPS + (unit - 1) * UNIT_STEPS)
                            act.wait_ge(turned, pair * (2 * PAIR_STEPS) + (2 * v + c + 1))
                            high, low = turned_views(unit, v, c)
                            nc.scalar.copy(high, t_ps[:, c]).then_inc(turned_high, 1)
                    if at < STEPS:
                        act.wait_ge(max_done, pair * PAIR_STEPS + (k + 1))
                        if at >= 2:
                            act.wait_ge(turned, pair * (2 * PAIR_STEPS) + 2 * (k - 1))
                        for t in range(STEP_TILES):
                            last = nc.scalar.activation(probs[:, k % 2, t, :], s_ps[:, k % 2, t, :], ACT.Exp,
                                                        bias=neg_max[:, k % 2, t:t + 1], scale=1.0)
                        last.then_inc(exp_done, 1)

                each_step(act, step)

        att.close()

        more_loaded = sem("more_loaded")
        chain = sem("chain")
        var_ready = sem("var_ready")
        root_done = sem("root_done")
        normed = sem("normed")
        x_turned = sem("x_turned")
        x_high = sem("x_high")
        x_low = sem("x_low")
        x_copied = sem("x_copied")
        residual_added = sem("residual_added")
        w1_loaded = sem("w1_loaded")
        w_high = sem("w_high")
        w2_loaded = sem("w2_loaded")
        logits_done = sem("logits_done")
        shifted = sem("shifted")
        exp_gates = sem("exp_gates")
        gates_done = sem("gates_done")
        g_turned = sem("g_turned")
        g_copied = [sem(f"g_copied{i}") for i in range(2)]
        first_stored = sem("first_stored")
        g_stored = sem("g_stored")
        gates_spread = [sem(f"gates_spread{i}") for i in range(2)]
        MORE = 5

        ffn = ExitStack()
        w2h = alloc(ffn, "w2h", [P, E, FC, D], F32R)
        w2l = alloc(ffn, "w2l", [P, E, FC, D], F32R)
        w1h = alloc(ffn, "w1h", [P, E, F], F32R)
        w1l = alloc(ffn, "w1l", [P, E, F], F32R)
        b1_sb = alloc(ffn, "b1_sb", [P, HN])
        xh = alloc(ffn, "xh", [P, TOK], F32R)
        xl = alloc(ffn, "xl", [P, TOK], F32R)
        gT = alloc(ffn, "gT", [E, TOK])
        b2_sb = alloc(ffn, "b2_sb", [E, D])
        HE = E // 2
        gate_sb = attn[:].rearrange("p (u e a) d -> p u e (a d)", u=2, e=HE)

        def spread_gates(sp, c, half):
            cols = gate_dram[half * HE:(half + 1) * HE, c * CHUNK:(c + 1) * CHUNK]
            sp.dma_start(gate_sb[:, half], cols.partition_broadcast(P)).then_inc(gates_spread[half], 16)

        with ExitStack() as st:
            w1_sb = alloc(st, "w1_sb", [P, E, F])
            w2_sb = alloc(st, "w2_sb", [P, E, FC, D])
            wg_sb = alloc(st, "wg_sb", [P, E])
            bg_sb = alloc(st, "bg_sb", [P, E])
            order = alloc(st, "order", [P, E])
            stats = alloc(st, "stats", [P, TILES, 6])
            mv = alloc(st, "mv", [P, TILES, 2])
            var = alloc(st, "var", [P, TILES])
            root = alloc(st, "root", [P, TILES])
            rstd = alloc(st, "rstd", [P, TILES])
            xfull = alloc(st, "xfull", [P, 2, CT, P])
            logit = alloc(st, "logit", [P, TILES, E])
            gate = alloc(st, "gate", [P, TILES, E])
            red = alloc(st, "red", [P, TILES])
            rest = alloc(st, "rest", [P, TILES, E])
            keep = alloc(st, "keep", [P, TILES, E])
            picked = alloc(st, "picked", [P, 2, TILES, E])
            place = alloc(st, "place", [P, TILES, E])
            xt_ps = psum(st, "xt_ps", [P, 4, CT, P])
            l_ps = psum(st, "l_ps", [P, 512])
            g_ps = psum(st, "g_ps", [E, 2, CHUNK])
            weights = [(w1l[:, e], w1_sb[:, e], w1h[:, e]) for e in range(E)]
            weights += [(w2l[:, e], w2_sb[:, e], w2h[:, e]) for e in range(E)]
            block = st.enter_context(nc.Block())

            @block.sync
            def _(sp):
                sp.wait_ge(x_loaded, 16)
                sp.dma_start(wg_sb[:], Wg).then_inc(more_loaded, 16)
                sp.dma_start(bg_sb[:], bg.partition_broadcast(P)).then_inc(more_loaded, 16)
                sp.dma_start(order[:], order_in).then_inc(more_loaded, 16)
                sp.dma_start(b1_sb[:], b1T).then_inc(more_loaded, 16)
                sp.dma_start(b2_sb[:], b2).then_inc(more_loaded, 16)
                sp.dma_start(w1_sb[:], W1.rearrange("e d f -> d e f")).then_inc(w1_loaded, 16)
                sp.dma_start(w2_sb[:], W2.rearrange("e (c p) d -> p e c d", p=P)).then_inc(w2_loaded, 16)
                sp.wait_ge(g_copied[0], 1)
                sp.dma_start(gate_dram[:, 0:CHUNK], gT[:, 0:CHUNK]).then_inc(first_stored, 16)
                sp.wait_ge(first_stored, 16)
                for half in range(2):
                    spread_gates(sp, 0, half)
                for part in range(2):
                    sp.wait_ge(g_copied[part], CHUNKS // 2)
                sp.dma_start(gate_dram[:, CHUNK:TOK], gT[:, CHUNK:TOK]).then_inc(g_stored, 16)

            @block.gpsimd
            def _(pool):
                pool.wait_ge(x_loaded, 16)
                for c in range(CHUNKS):
                    tiles = slice(c * CT, (c + 1) * CT)
                    nc.gpsimd.tensor_tensor(attn[:, tiles, :], attn[:, tiles, :], x_sb[:, tiles, :],
                                            ALU.add).then_inc(residual_added, 1)

                def weight_low(n):
                    low, raw, high = weights[n]
                    pool.wait_ge(w_high, n + 1)
                    nc.gpsimd.tensor_tensor(low, raw, high.bitcast(F32), ALU.subtract)

                for c in range(CHUNKS):
                    pool.wait_ge(x_high, c + 1)
                    pool.wait_ge(x_copied, c + 1)
                    cols = slice(c * CHUNK, (c + 1) * CHUNK)
                    nc.gpsimd.tensor_tensor(xl[:, cols], xfull[:, c % 2].rearrange("p a b -> p (a b)"),
                                            xh[:, cols].bitcast(F32), ALU.subtract).then_inc(x_low, 1)
                    if c >= 2:
                        weight_low(c - 2)
                for n in range(CHUNKS - 2, 2 * E):
                    weight_low(n)

            @block.vector
            def _(dve):
                links = [0]

                def link(ins):
                    links[0] += 1
                    ins.then_inc(chain, 1)
                    dve.wait_ge(chain, links[0])

                def spread(row):
                    return row.unsqueeze(2).to_broadcast([P, TILES, E])

                def moments(c):
                    tiles = slice(c * CT, (c + 1) * CT)
                    dve.wait_ge(residual_added, c + 1)
                    for t in range(c * CT, (c + 1) * CT):
                        last = nc.vector.bn_stats(stats[:, t, :], attn[:, t, :])
                    link(last)
                    for t in range(c * CT, (c + 1) * CT):
                        last = nc.vector.bn_aggr(mv[:, t, :], stats[:, t, :])
                    link(last)
                    nc.vector.tensor_scalar(var[:, tiles], mv[:, tiles, 1], EPS, None, ALU.add).then_inc(var_ready, 1)

                def normalise(c):
                    tiles = slice(c * CT, (c + 1) * CT)
                    dve.wait_ge(root_done, c + 1)
                    link(nc.vector.reciprocal(rstd[:, tiles], root[:, tiles]))
                    for t in range(c * CT, (c + 1) * CT):
                        last = nc.vector.tensor_scalar(x_sb[:, t, :], attn[:, t, :], mv[:, t, 0:1], rstd[:, t:t + 1],
                                                       ALU.subtract, ALU.mult)
                    last.then_inc(normed, 1)

                for c in range(CHUNKS + 1):
                    if c < CHUNKS:
                        moments(c)
                    if c:
                        normalise(c - 1)
                dve.wait_ge(more_loaded, 16 * MORE)
                dve.wait_ge(logits_done, CHUNKS)
                link(nc.vector.tensor_tensor(logit[:], l_ps[:, 0:TILES * E].rearrange("p (t e) -> p t e", e=E),
                                             bg_sb[:].unsqueeze(1).to_broadcast([P, TILES, E]), ALU.add))
                link(nc.vector.tensor_reduce(red[:], logit[:], axis=AX.X, op=ALU.max))
                nc.vector.tensor_tensor(logit[:], logit[:], spread(red[:]), ALU.subtract).then_inc(shifted, 1)
                dve.wait_ge(exp_gates, 1)
                link(nc.vector.tensor_reduce(red[:], gate[:], axis=AX.X, op=ALU.add))
                link(nc.vector.reciprocal(red[:], red[:]))
                link(nc.vector.tensor_tensor(gate[:], gate[:], spread(red[:]), ALU.mult))
                for n in range(2):
                    source = rest if n else gate
                    link(nc.vector.tensor_reduce(red[:], source[:], axis=AX.X, op=ALU.max))
                    link(nc.vector.tensor_tensor(place[:], source[:], spread(red[:]), ALU.is_equal))
                    link(nc.vector.scalar_tensor_tensor(place[:], place[:], -float(E),
                                                        order[:].unsqueeze(1).to_broadcast([P, TILES, E]),
                                                        ALU.mult, ALU.add))
                    link(nc.vector.tensor_reduce(red[:], place[:], axis=AX.X, op=ALU.min))
                    link(nc.vector.tensor_tensor(picked[:, n], place[:], spread(red[:]), ALU.is_equal))
                    if n == 0:
                        link(nc.vector.scalar_tensor_tensor(rest[:], picked[:, 0], -2.0, gate[:], ALU.mult, ALU.add))
                link(nc.vector.tensor_tensor(keep[:], picked[:, 0], picked[:, 1], ALU.add))
                nc.vector.tensor_tensor(gate[:], gate[:], keep[:], ALU.mult).then_inc(gates_done, 1)
                for c in range(1, CHUNKS, 2):
                    dve.wait_ge(g_turned, c + 1)
                    nc.vector.tensor_copy(gT[:, c * CHUNK:(c + 1) * CHUNK], g_ps[:, 1, :]).then_inc(g_copied[1], 1)

            @block.scalar
            def _(act):
                def take_root(c):
                    act.wait_ge(var_ready, c + 1)
                    tiles = slice(c * CT, (c + 1) * CT)
                    nc.scalar.activation(root[:, tiles], var[:, tiles], ACT.Sqrt).then_inc(root_done, 1)

                def high_parts(first, last):
                    for n in range(first, last):
                        if n % E == 0:
                            act.wait_ge(w2_loaded if n else w1_loaded, 16)
                        low, raw, high = weights[n]
                        nc.scalar.copy(high, raw).then_inc(w_high, 1)

                for c in range(2):
                    take_root(c)
                for c in range(CHUNKS):
                    if c + 2 < CHUNKS:
                        take_root(c + 2)
                    act.wait_ge(x_turned, c + 1)
                    if c >= 2:
                        act.wait_ge(logits_done, c - 1)
                        act.wait_ge(x_low, c - 1)
                    nc.scalar.copy(xh[:, c * CHUNK:(c + 1) * CHUNK],
                                   xt_ps[:, c % 4].rearrange("p a b -> p (a b)")).then_inc(x_high, 1)
                    nc.scalar.copy(xfull[:, c % 2], xt_ps[:, c % 4]).then_inc(x_copied, 1)
                    if c >= 2:
                        high_parts(3 * (c - 2), min(3 * (c - 1), 2 * E))
                act.wait_ge(shifted, 1)
                nc.scalar.activation(gate[:], logit[:], ACT.Exp).then_inc(exp_gates, 1)
                for c in range(0, CHUNKS, 2):
                    act.wait_ge(g_turned, c + 1)
                    nc.scalar.copy(gT[:, c * CHUNK:(c + 1) * CHUNK], g_ps[:, 0, :]).then_inc(g_copied[0], 1)

            @block.tensor
            def _(pe):
                def logits(c):
                    pe.wait_ge(x_copied, c + 1)
                    for t in range(CT):
                        n = c * CT + t
                        last = nc.tensor.matmul(l_ps[:, n * E:(n + 1) * E], xfull[:, c % 2, t, :], wg_sb[:],
                                                start=True, stop=True)
                    last.then_inc(logits_done, 1)

                pe.wait_ge(more_loaded, 16 * MORE)
                for c in range(CHUNKS):
                    pe.wait_ge(normed, c + 1)
                    if c >= 4:
                        pe.wait_ge(x_high, c - 3)
                        pe.wait_ge(x_copied, c - 3)
                    for t in range(CT):
                        last = nc.tensor.transpose(xt_ps[:, c % 4, t, :], x_sb[:, CT * c + t, :], ident[:])
                    last.then_inc(x_turned, 1)
                    if c:
                        logits(c - 1)
                logits(CHUNKS - 1)
                pe.wait_ge(gates_done, 1)
                for c in range(CHUNKS):
                    if c >= 2:
                        pe.wait_ge(g_copied[c % 2], c // 2)
                    for t in range(CT):
                        last = nc.tensor.transpose(g_ps[:, c % 2, t * P:(t + 1) * P],
                                                   gate[:, CT * c + t, :], ident[:])
                    last.then_inc(g_turned, 1)

        h_done = sem("h_done")
        h_gated = sem("h_gated")
        h_relu_done = sem("h_relu_done")
        h_low_done = sem("h_low_done")
        h_used = sem("h_used")
        y_copied = sem("y_copied")
        y_turned = sem("y_turned")
        y_read = sem("y_read")
        chain4 = sem("chain4")
        var4 = sem("var4")
        root4 = sem("root4")
        out_ready = sem("out_ready")
        out_stored = [sem(f"out_stored{i}") for i in range(2)]
        LAGH = 5
        HBUF = 8
        COPY_AT = 6
        TURN_AT = 8
        NORM_AT = 11
        VAR_AT = 15
        ROOT_AT = 18
        SCALE_AT = (22, 26)
        LINKS = 3

        with ExitStack() as st:
            h_sb = alloc(st, "h_sb", [P, 4, CHUNK])
            h_full = alloc(st, "h_full", [P, 2, CHUNK])
            h_high = alloc(st, "h_high", [P, HBUF, CHUNK], F32R)
            h_low = alloc(st, "h_low", [P, HBUF, CHUNK], F32R)
            y_sb = alloc(st, "y_sb", [P, CHUNK])
            z_sb = alloc(st, "z_sb", [P, CT, D])
            out_sb = alloc(st, "out_sb", [P, 2, CT, D])
            stats4 = alloc(st, "stats4", [P, CT, 6])
            mv4 = alloc(st, "mv4", [P, CT, 2])
            var_sb = alloc(st, "var_sb", [P, CT])
            root_sb = alloc(st, "root_sb", [P, CT])
            rstd_sb = alloc(st, "rstd_sb", [P, CT])
            pause = alloc(st, "pause", [P, 1])
            h_ps = psum(st, "h_ps", [P, 4, CHUNK])
            y_ps = psum(st, "y_ps", [P, 2, CHUNK])
            yt_ps = psum(st, "yt_ps", [P, CT, P])
            block = st.enter_context(nc.Block())

            def each_chunk(eng, chunk):
                for s in range(2):
                    chunk(0, s, s > 0, True)
                with eng.Fori(1, CHUNKS // 2) as pair:
                    for s in range(2):
                        chunk(pair, s, True, True)
                chunk(CHUNKS // 2, 0, True, False)

            @block.tensor
            def _(pe):
                def chunk(pair, s, before, now):
                    c = pair * 2 + s
                    cols = bass.ds(c * CHUNK, CHUNK)
                    for n in range(HN):
                        if now:
                            e = n // FC
                            part = slice((n % FC) * P, (n % FC + 1) * P)
                            if before or n >= 4:
                                pe.wait_ge(h_gated, c * HN + (n - 3))
                            if n == LAGH and (not isinstance(c, int) or c >= 2):
                                pe.wait_ge(y_copied, c - 1)
                            o = h_ps[:, n % 4, :]
                            nc.tensor.matmul(o, w1h[:, e, part], xh[:, cols], start=True, stop=False)
                            nc.tensor.matmul(o, w1h[:, e, part], xl[:, cols], start=False, stop=False)
                            nc.tensor.matmul(o, w1l[:, e, part], xh[:, cols], start=False,
                                             stop=True).then_inc(h_done, 1)
                        if n >= LAGH and now or n < LAGH and before:
                            m = (n - LAGH) % HN
                            slot = s if n >= LAGH else 1 - s
                            o = y_ps[:, slot, :]
                            if m == 0:
                                nc.tensor.matmul(o, b2_sb[:], gT[:, cols], start=True, stop=False)
                            pe.wait_ge(h_low_done, c * HN + (n - LAGH + 1))
                            w2_high, w2_low = [w[:, m // FC, m % FC, :] for w in (w2h, w2l)]
                            nc.tensor.matmul(o, w2_high, h_high[:, m % HBUF, :], start=False, stop=False)
                            nc.tensor.matmul(o, w2_low, h_high[:, m % HBUF, :], start=False, stop=False)
                            nc.tensor.matmul(o, w2_high, h_low[:, m % HBUF, :], start=False,
                                             stop=m == HN - 1).then_inc(h_used, 1)
                        if n == TURN_AT and before:
                            pe.wait_ge(y_copied, c)
                            if not isinstance(c, int) or c > 1:
                                pe.wait_ge(y_read, c - 1)
                            for t in range(CT):
                                last = nc.tensor.transpose(yt_ps[:, t, :], y_sb[:, t * P:(t + 1) * P], ident[:])
                            last.then_inc(y_turned, 1)

                each_chunk(pe, chunk)

            @block.scalar
            def _(act):
                def chunk(pair, s, before, now):
                    c = pair * 2 + s
                    for n in range(HN):
                        if now:
                            act.wait_ge(h_gated, c * HN + (n + 1))
                            if before or n >= HBUF:
                                act.wait_ge(h_used, c * HN + (n - HBUF + 1))
                            nc.scalar.activation(h_high[:, n % HBUF, :], h_sb[:, n % 4, :], ACT.Relu)
                            if before or n >= 2:
                                act.wait_ge(h_low_done, c * HN + (n - 1))
                            nc.scalar.activation(h_full[:, n % 2, :], h_sb[:, n % 4, :], ACT.Relu).then_inc(
                                h_relu_done, 1)
                        if n == COPY_AT and before:
                            act.wait_ge(h_used, c * HN)
                            if not isinstance(c, int) or c > 1:
                                act.wait_ge(y_turned, c - 1)
                            nc.scalar.copy(y_sb[:], y_ps[:, 1 - s, :]).then_inc(y_copied, 1)
                        if n == ROOT_AT and before:
                            act.wait_ge(var4, c)
                            nc.scalar.activation(root_sb[:], var_sb[:], ACT.Sqrt).then_inc(root4, 1)

                each_chunk(act, chunk)

            @block.vector
            def _(dve):
                def residual(c):
                    dve.wait_ge(y_turned, c)
                    nc.vector.tensor_tensor(z_sb[:], yt_ps[:], x_sb[:, bass.ds((c - 1) * CT, CT), :],
                                            ALU.add).then_inc(y_read, 1)
                    dve.wait_ge(y_read, c)
                    for t in range(CT):
                        last = nc.vector.bn_stats(stats4[:, t, :], z_sb[:, t, :])
                    last.then_inc(chain4, 1)

                def variance(c):
                    link = (c - 1) * LINKS
                    dve.wait_ge(chain4, link + 1)
                    nc.vector.memset(pause[:], 0.0)
                    for t in range(CT):
                        last = nc.vector.bn_aggr(mv4[:, t, :], stats4[:, t, :])
                    last.then_inc(chain4, 1)
                    dve.wait_ge(chain4, link + 2)
                    nc.vector.tensor_scalar(var_sb[:], mv4[:, :, 1], EPS, None, ALU.add).then_inc(var4, 1)

                def scale(pair, c, s, tiles):
                    link = (c - 1) * LINKS
                    if tiles[0] == 0:
                        dve.wait_ge(root4, c)
                        nc.vector.reciprocal(rstd_sb[:], root_sb[:]).then_inc(chain4, 1)
                        dve.wait_ge(chain4, link + 3)
                        if not isinstance(c, int) or c > 2:
                            dve.wait_ge(out_stored[0], pair * 16)
                    for t in tiles:
                        last = nc.vector.tensor_scalar(out_sb[:, 1 - s, t, :], z_sb[:, t, :], mv4[:, t, 0:1],
                                                       rstd_sb[:, t:t + 1], ALU.subtract, ALU.mult)
                    if tiles[-1] == CT - 1:
                        last.then_inc(out_ready, 1)

                def chunk(pair, s, before, now):
                    c = pair * 2 + s
                    for n in range(HN):
                        if now:
                            dve.wait_ge(h_done, c * HN + (n + 1))
                            if n % (HE * FC) == 0:
                                dve.wait_ge(gates_spread[n // (HE * FC)], c * 16 + 16)
                            if before or n >= 4:
                                dve.wait_ge(h_relu_done, c * HN + (n - 3))
                            nc.vector.scalar_tensor_tensor(h_sb[:, n % 4, :], h_ps[:, n % 4, :], b1_sb[:, n:n + 1],
                                                           gate_sb[:, n // (HE * FC), (n // FC) % HE, :], ALU.add,
                                                           ALU.mult).then_inc(h_gated, 1)
                        if n == NORM_AT and before:
                            residual(c)
                        if n == VAR_AT and before:
                            variance(c)
                        if n in SCALE_AT and before:
                            first = SCALE_AT.index(n) * (CT // 2)
                            scale(pair, c, s, range(first, first + CT // 2))

                each_chunk(dve, chunk)

            @block.gpsimd
            def _(pool):
                def chunk(pair, s, before, now):
                    c = pair * 2 + s
                    if not now:
                        return
                    for n in range(HN):
                        pool.wait_ge(h_relu_done, c * HN + (n + 1))
                        if before or n >= HBUF:
                            pool.wait_ge(h_used, c * HN + (n - HBUF + 1))
                        nc.gpsimd.tensor_tensor(h_low[:, n % HBUF, :], h_full[:, n % 2, :],
                                                h_high[:, n % HBUF, :].bitcast(F32), ALU.subtract).then_inc(h_low_done, 1)

                each_chunk(pool, chunk)

            @block.sync
            def _(sp):
                def next_gates(c, half):
                    sp.wait_ge(h_gated, (c - 1) * HN + (half + 1) * HE * FC)
                    spread_gates(sp, c, half)

                sp.wait_ge(g_stored, 16)
                for c in range(CHUNKS + 1):
                    if c < CHUNKS - 1:
                        next_gates(c + 1, 0)
                    if c:
                        if c > 1:
                            sp.wait_ge(out_stored[c % 2], 16 * (c // 2))
                        sp.wait_ge(out_ready, c)
                        sp.dma_start(out[(c - 1) * CT:c * CT].rearrange("t p d -> p t d"),
                                     out_sb[:, (c - 1) % 2]).then_inc(out_stored[(c - 1) % 2], 16)
                    if c < CHUNKS - 1:
                        next_gates(c + 1, 1)
                for s in range(2):
                    sp.wait_ge(out_stored[s], 16 * (CHUNKS // 2))

        ffn.close()


def sinusoids():
    inv = np.float32(1.0) / np.float32(10000.0) ** (np.arange(0, D, 2, dtype=np.float32) / np.float32(D))
    ang = np.arange(-(L - 1), L, dtype=np.float32)[:, None] * inv[None, :].astype(np.float32)
    emb = np.zeros((2 * L - 1, D), np.float32)
    emb[:, 0::2] = np.sin(ang)
    emb[:, 1::2] = np.cos(ang)
    low = np.zeros((D, REL_PAD), np.float32)
    up = np.zeros((D, REL_PAD), np.float32)
    low[:, 0:L] = emb.T[:, L - 1:2 * L - 1]
    up[:, L + 1:2 * L - 1] = emb.T[:, 0:L - 2]
    return low, up


def kernel(L0_attn_w, L0_attn_Wq, L0_attn_Wk, L0_attn_Wv, L0_attn_Wr, L0_attn_u_bias, L0_attn_v_bias, L0_ffn_Wg,
           L0_ffn_bg, L0_ffn_W1, L0_ffn_b1, L0_ffn_W2, L0_ffn_b2):
    import concourse.bacc as bacc
    from concourse.bass_utils import run_bass_kernel_spmd

    w = np.asarray(L0_attn_w)
    low, up = sinusoids()
    arrays = {
        "w_tok": w.reshape(B, NHI, HALF, LO, D).transpose(0, 2, 1, 3, 4).reshape(TILES, P, D),
        "wT": w.reshape(TOK, D).T,
        "WqT": np.asarray(L0_attn_Wq).T,
        "WkT": np.asarray(L0_attn_Wk).T,
        "WvT": np.asarray(L0_attn_Wv).T,
        "WrT": np.asarray(L0_attn_Wr).T,
        "u_bias": np.asarray(L0_attn_u_bias).reshape(D, 1),
        "v_bias": np.asarray(L0_attn_v_bias).reshape(D, 1),
        "sin_low": low,
        "sin_up": up,
        "ident_in": np.eye(P, dtype=np.float32),
        "order_in": np.tile(np.arange(E, 2 * E, dtype=np.float32), (P, 1)),
        "Wg": np.asarray(L0_ffn_Wg),
        "bg": np.asarray(L0_ffn_bg),
        "W1": np.asarray(L0_ffn_W1),
        "b1T": np.asarray(L0_ffn_b1).reshape(HN, P).T,
        "W2": np.asarray(L0_ffn_W2),
        "b2": np.asarray(L0_ffn_b2),
    }
    arrays = {f"{n}_dram": np.ascontiguousarray(a) for n, a in arrays.items()}
    nc = bacc.Bacc("TRN2", target_bir_lowering=False, num_devices=1)
    args = [nc.dram_tensor(n, a.shape, F32, kind="ExternalInput").ap() for n, a in arrays.items()]
    out = nc.dram_tensor("out_dram", (TILES, P, D), F32, kind="ExternalOutput").ap()
    attention_moe_kernel(nc, *args, out)
    r = run_bass_kernel_spmd(nc, [arrays], core_ids=[0])
    y = r.results[0]["out_dram"]
    return y.reshape(B, HALF, NHI, LO, D).transpose(0, 2, 1, 3, 4).reshape(B, L, D)
```
